# Optimizing a Trainium2 kernel written in Bass

```python
import numpy as np
import jax
import jax.numpy as jnp

def _softmax(x, axis=-1):
    return jax.nn.softmax(x, axis=axis)

def _gelu(x):
    return jax.nn.gelu(x, approximate=True)

def _silu(x):
    return jax.nn.silu(x)

def _sigmoid(x):
    return jax.nn.sigmoid(x)

def _layernorm(x, axis=-1, eps=1e-05):
    m = jnp.mean(x, axis=axis, keepdims=True)
    v = jnp.var(x, axis=axis, keepdims=True)
    return (x - m) / jnp.sqrt(v + eps)

def _scatter_add(tgt, idx, src, axis=0):
    return tgt.at[idx].add(src)

def _segment_sum(src, seg, n):
    return jax.ops.segment_sum(src, seg, n)
kernel_name = 'mk_flamingo_gated_d1_seqx_r4_48e99e'

def setup_inputs(seed: int=0):
    np.random.seed(seed)
    _w = jnp.asarray

    def _rec_inputs():
        import jax
        import jax.numpy as jnp
        _rk = jax.random.key(seed)
        x = -0.0003929 + 0.9999 * jax.random.normal(jax.random.fold_in(_rk, 1), (4, 1024, 256), jnp.float32)
        _lenS = 1024 - jax.random.randint(jax.random.fold_in(_rk, 7), (4,), 0, max(1, 1024 // 4) + 1, jnp.int32)
        _lenS2 = 77 - jax.random.randint(jax.random.fold_in(_rk, 8), (4,), 0, max(1, 77 // 4) + 1, jnp.int32)
        _ctx_1024P = jax.random.normal(jax.random.fold_in(_rk, 11), (4, 16, 256), jnp.float32)
        _ctx_1024c = jax.random.dirichlet(jax.random.fold_in(_rk, 511), 0.3 * jnp.ones((16,), jnp.float32), (4, 77))
        _ctx_1024t = jnp.einsum('bsk,bkd->bsd', _ctx_1024c, _ctx_1024P)
        _ctx_1024t = _ctx_1024t * jax.lax.rsqrt(jnp.mean(jnp.square(_ctx_1024t)) + 1e-12) * 0.953939
        ctx_1024 = 2.81802e-05 + 1.00001 * (_ctx_1024t + 0.3 * jax.random.normal(jax.random.fold_in(_rk, 611), (4, 77, 256), jnp.float32))
        _g = jax.random.normal(jax.random.fold_in(_rk, 9001), (2, 1), jnp.float32)
        _g = jnp.sign(_g) * jnp.maximum(jnp.abs(_g), 1.0) + (_g == 0) * 1.0
        g_xattn = _g[0]
        g_ffn = _g[1]
        return (x, ctx_1024, _lenS2, g_xattn, g_ffn)
    x, ctx_1024, _lenS2, g_xattn, g_ffn = _rec_inputs()

    def _L0_xattn_setup():
        import jax, jax.numpy as jnp
        import numpy as np
        NEG = -10000000000000.0
        key = jax.random.key(seed)
        ks = jax.random.split(key, 7)
        B, L, D, E = (8, 512, 256, 256)
        Q = jax.random.normal(ks[0], (B, L, D), dtype=jnp.float32)
        K = jax.random.normal(ks[1], (B, L, D), dtype=jnp.float32)
        V = jax.random.normal(ks[2], (B, L, D), dtype=jnp.float32)
        query_pad_idxs = jax.random.randint(ks[3], (B,), 0, L)
        key_pad_idxs = jax.random.randint(ks[4], (B,), 0, L)
        W = jax.random.normal(ks[5], (E, D), dtype=jnp.float32) / np.sqrt(D)
        b = jax.random.normal(ks[6], (E,), dtype=jnp.float32) * 0.01
        return {'Q': Q, 'K': K, 'V': V, 'query_pad_idxs': query_pad_idxs, 'key_pad_idxs': key_pad_idxs, 'W': W, 'b': b}
    _L0_xattn_all = _L0_xattn_setup()
    _L0_xattn_in = {k: v for k, v in _L0_xattn_all.items() if k in ('W', 'b')}
    del _L0_xattn_all

    def _L0_ffn_setup():
        import jax, jax.numpy as jnp
        import numpy as np
        from jax import lax
        DIM = 256
        HID = 512
        E = 8
        K = 2
        B, T = (2, 128)
        key = jax.random.key(seed)
        ks = jax.random.split(key, 5)
        scale = 1.0 / np.sqrt(DIM)
        x = jax.random.normal(ks[0], (B, T, DIM), dtype=jnp.float32)
        router_w = jax.random.normal(ks[1], (E, DIM), dtype=jnp.float32) * scale
        w_gate = jax.random.normal(ks[2], (E, HID, DIM), dtype=jnp.float32) * scale
        w_up = jax.random.normal(ks[3], (E, HID, DIM), dtype=jnp.float32) * scale
        w_down = jax.random.normal(ks[4], (E, DIM, HID), dtype=jnp.float32) * (1.0 / np.sqrt(HID))
        return {'x': x, 'router_w': router_w, 'w_gate': w_gate, 'w_up': w_up, 'w_down': w_down}
    _L0_ffn_all = _L0_ffn_setup()
    _L0_ffn_in = {k: v for k, v in _L0_ffn_all.items() if k in ('router_w', 'w_gate', 'w_up', 'w_down')}
    del _L0_ffn_all
    return {'x': x, 'ctx_1024': ctx_1024, '_lenS2': _lenS2, 'g_xattn': g_xattn, 'g_ffn': g_ffn, 'L0_xattn_W': _L0_xattn_in['W'], 'L0_xattn_b': _L0_xattn_in['b'], 'L0_ffn_router_w': _L0_ffn_in['router_w'], 'L0_ffn_w_gate': _L0_ffn_in['w_gate'], 'L0_ffn_w_up': _L0_ffn_in['w_up'], 'L0_ffn_w_down': _L0_ffn_in['w_down']}

def reference(x, ctx_1024, _lenS2, g_xattn, g_ffn, L0_xattn_W, L0_xattn_b, L0_ffn_router_w, L0_ffn_w_gate, L0_ffn_w_up, L0_ffn_w_down):
    import jax
    import jax.numpy as jnp

    def _L0_xattn_ref(Q, K, V, query_pad_idxs, key_pad_idxs, W, b):
        import jax, jax.numpy as jnp
        import numpy as np
        NEG = -10000000000000.0
        B, Lq, D = Q.shape
        Lk = K.shape[1]
        scale = 1.0 / jnp.sqrt(jnp.asarray(D, dtype=Q.dtype))
        scores = jnp.einsum('bqd,bkd->bqk', Q, K) * scale
        qpos = jnp.arange(Lq)[None, :, None]
        kpos = jnp.arange(Lk)[None, None, :]
        mask = (qpos >= query_pad_idxs[:, None, None]) & (kpos >= key_pad_idxs[:, None, None])
        scores = jnp.where(mask, jnp.asarray(NEG, scores.dtype), scores)
        attn = jax.nn.softmax(scores, axis=2)
        out = jnp.einsum('bqk,bkd->bqd', attn, V)
        return out @ W.T + b

    def _L0_ffn_ref(x, router_w, w_gate, w_up, w_down):
        import jax, jax.numpy as jnp
        import numpy as np
        from jax import lax
        DIM = 256
        HID = 512
        E = 8
        K = 2
        B, T = (2, 128)
        Bb, Tt, D = x.shape
        N = Bb * Tt
        xf = x.reshape(N, D)
        logits = xf @ router_w.T
        routing = jax.nn.softmax(logits, axis=-1)
        top_w, top_i = lax.top_k(routing, K)
        top_w = top_w / jnp.sum(top_w, axis=-1, keepdims=True)
        combine = jnp.zeros((N, E), dtype=x.dtype)
        combine = combine.at[jnp.arange(N)[:, None], top_i].add(top_w)
        g = jnp.einsum('nd,ehd->neh', xf, w_gate)
        u = jnp.einsum('nd,ehd->neh', xf, w_up)
        h = jax.nn.silu(g) * u
        y = jnp.einsum('neh,edh->ned', h, w_down)
        out = jnp.einsum('ned,ne->nd', y, combine)
        return out.reshape(Bb, Tt, D)
    x = x + jnp.tanh(g_xattn[0]) * _L0_xattn_ref(_layernorm(x, axis=-1), ctx_1024, ctx_1024, _lenS2, _lenS2, L0_xattn_W, L0_xattn_b)
    x = x + jnp.tanh(g_ffn[0]) * _L0_ffn_ref(_layernorm(x, axis=-1), L0_ffn_router_w, L0_ffn_w_gate, L0_ffn_w_up, L0_ffn_w_down)
    return x

_drawn_inputs = setup_inputs


def setup_inputs(seed=0):
    import zlib

    import numpy as np

    out = dict(_drawn_inputs(seed))
    spreads = {}
    factors = {}
    for name, (base, spread) in spreads.items():
        noise = np.random.default_rng([zlib.crc32(name.encode()), seed]).standard_normal(out[name].shape)
        drawn = base * np.exp(spread * noise) if base else spread * noise
        out[name] = jnp.asarray(drawn.astype(out[name].dtype))
    for name, factor in factors.items():
        out[name] = (out[name] * factor).astype(out[name].dtype)
    return out
```

```python
import concourse.bass as bass
from concourse import mybir
from contextlib import ExitStack

F32 = mybir.dt.float32
BF16 = mybir.dt.bfloat16
I32 = mybir.dt.int32
U32 = mybir.dt.uint32
ALU = mybir.AluOpType
ACT = mybir.ActivationFunctionType
AX = mybir.AxisListType

P = 128
BATCH, SEQ, D = 4, 1024, 256
CTX = 77
NE, HID, TOPK = 8, 512, 2
N = BATCH * SEQ
DC, HC = D // P, HID // P
G = 4
GROUPS = N // (G * P)
HALF = GROUPS // 2
NT = N // P
QT = SEQ // P
KR = 96
OW = D + NE
EPS = 1e-5
MASKED = -float(2 ** 100)

REGION = N + P
TILES = (TOPK * N - NE) // P + NE
SPARE = TILES - TOPK * N // P
ROW = D + 1 + NE
TOK, CW = D, D + 1
XR = 4
TURNS = (TILES - 2) // XR
GUW, DW = DC * 2 * HID, HC * D


def moe_flamingo(nc, x, xT, ctx_rows, ctxT, lens, g_x, g_f, w_rows, wT, b_row, b_col, router, w_gateT,
                 w_upT, w_downT, out):
    sorted_rows = nc.dram_tensor("sorted_rows", (NE * REGION + SPARE * P, ROW), F32, kind="Internal").ap()
    es = ExitStack()
    with es:
        def sb(name, shape, dt=F32, stack=es):
            return stack.enter_context(nc.sbuf_tensor(name, shape, dt))

        def pb(name, shape, stack):
            return stack.enter_context(nc.psum_tensor(name, shape, F32))

        def sem(name):
            return es.enter_context(nc.semaphore(name))

        WGU = sb("WGU", [P, NE * GUW])
        WD = sb("WD", [P, NE * DW])
        ident = sb("ident", [P, P])
        gates = sb("gates", [P, 2])
        tile_expert = sb("tile_expert", [1, TILES], I32)
        tile_row = sb("tile_row", [1, TILES], I32)
        pad_row = sb("pad_row", [1, NE], I32)
        pad_tile = sb("pad_tile", [P, ROW])

        a = ExitStack()
        xg = sb("xg", [P, 2, G, D], F32, a)
        xTg = sb("xTg", [P, 2, DC, G * P], F32, a)
        pay = sb("pay", [P, 2, G, ROW], F32, a)
        kr = sb("kr", [KR, BATCH, D], F32, a)
        krT = sb("krT", [P, BATCH, DC, KR], F32, a)
        ctxT_sb = sb("ctxT_sb", [P, DC, BATCH * CTX], F32, a)
        w_sb = sb("w_sb", [P, DC, D], F32, a)
        wT_sb = sb("wT_sb", [P, DC, OW], F32, a)
        brow = sb("brow", [1, OW], F32, a)
        bcol = sb("bcol", [P, DC], F32, a)
        ones_row = sb("ones_row", [1, CTX], F32, a)
        vw = sb("vw", [CTX, BATCH, OW], F32, a)
        kst = sb("kst", [KR, BATCH, 6], F32, a)
        kmv = sb("kmv", [KR, BATCH, 2], F32, a)
        lens_i = sb("lens_i", [P, BATCH], I32, a)
        lens_f = sb("lens_f", [P, BATCH], F32, a)
        graw = sb("graw", [P, 2], F32, a)
        kpos = sb("kpos", [P, CTX], F32, a)
        qpos = sb("qpos", [P, QT], F32, a)
        kmask = sb("kmask", [P, BATCH * CTX], F32, a)
        qmask = sb("qmask", [P, NT], F32, a)
        tri = sb("tri", [P, P], BF16, a)
        ones = sb("ones", [P, P], BF16, a)
        minus_half = sb("minus_half", [P, G], F32, a)
        iota_e = sb("iota_e", [P, NE], F32, a)
        region = sb("region", [P, NE], F32, a)
        tok = sb("tok", [P, NT], I32, a)
        st1 = sb("st1", [P, G, 6], F32, a)
        mv1 = sb("mv1", [P, G, 2], F32, a)
        ve1 = sb("ve1", [P, 2, G], F32, a)
        sc1 = sb("sc1", [P, 2, G], F32, a)
        sm = sb("sm", [P, 2, G, CTX], F32, a)
        mx = sb("mx", [P, G], F32, a)
        nb = sb("nb", [P, 2, G], F32, a)
        sr = sb("sr", [P, 2, G, NE], F32, a)
        ex = sb("ex", [P, 2, G, CTX], F32, a)
        rs = sb("rs", [P, 2, G], F32, a)
        eT = sb("eT", [CTX, G * P], F32, a)
        rg = sb("rg", [P, G], F32, a)
        rgt = sb("rgt", [P, G], F32, a)
        lg0 = sb("lg0", [P, G, NE], F32, a)
        lg1 = sb("lg1", [P, G, NE], F32, a)
        lg = sb("lg", [P, G, NE], F32, a)
        st2 = sb("st2", [P, G, 6], F32, a)
        mv2 = sb("mv2", [P, G, 2], F32, a)
        ve2 = sb("ve2", [P, G], F32, a)
        rstd2 = sb("rstd2", [P, G], F32, a)
        nmr2 = sb("nmr2", [P, G], F32, a)
        m8 = sb("m8", [P, G, NE], F32, a)
        mi = sb("mi", [P, G, NE], U32, a)
        oh = sb("oh", [P, TOPK, G, NE], F32, a)
        picks = sb("picks", [P, G, NE], BF16, a)
        npicks = sb("npicks", [P, NE], F32, a)
        carry = sb("carry", [P, NE], BF16, a)
        dl = sb("dl", [P, G], F32, a)
        ed = sb("ed", [P, G], F32, a)
        ed1 = sb("ed1", [P, G], F32, a)
        rw = sb("rw", [P, G], F32, a)
        wk = sb("wk", [P, TOPK, G], F32, a)
        cw = sb("cw", [P, TOPK, G, NE], F32, a)
        place = sb("place", [P, G, NE], F32, a)
        po = sb("po", [P, TOPK, G, NE], F32, a)
        slot = sb("slot", [P, 2, TOPK, G], I32, a)
        J = sb("J", [1, TILES], F32, a)
        cnt = sb("cnt", [1, NE], F32, a)
        nti = sb("nti", [1, NE], I32, a)
        nts = sb("nts", [1, NE], I32, a)
        ntf = sb("ntf", [1, NE], F32, a)
        cum = sb("cum", [1, NE], F32, a)
        one8 = sb("one8", [1, NE], F32, a)
        past = sb("past", [1, TILES, NE], F32, a)
        pastn = sb("pastn", [1, TILES, NE], F32, a)
        tex = sb("tex", [1, TILES], F32, a)
        before = sb("before", [1, TILES], F32, a)
        rel = sb("rel", [1, TILES], F32, a)
        rel128 = sb("rel128", [1, TILES], F32, a)
        S = pb("S", [P, 2, 512], a)
        ET = pb("ET", [P, 512], a)
        R = pb("R", [P, 512], a)
        O = pb("O", [P, G, 512], a)
        a.close()

        xt = sb("xt", [P, XR, ROW])
        xtT = sb("xtT", [P, 2, D])
        hid = sb("hid", [P, 2, HID])
        hT = sb("hT", [P, HID])
        y = sb("y", [P, 2, D])
        XT = pb("XT", [P, 2, 512], es)
        GT = pb("GT", [P, 512], es)
        UP = pb("UP", [P, 512], es)
        HT = pb("HT", [P, 512], es)
        Y = pb("Y", [P, 2, 512], es)

        kr_zeroed = sem("kr_zeroed")
        small_loaded = sem("small_loaded")
        pool_consts = sem("pool_consts")
        pads_ready = sem("pads_ready")
        setup_steps = sem("setup_steps")
        keys_centred = sem("keys_centred")
        krT_ready = sem("krT_ready")
        krT_copied = sem("krT_copied")
        wr_ready = sem("wr_ready")
        wr_copied = sem("wr_copied")
        vw_ready = sem("vw_ready")
        vw_copied = sem("vw_copied")
        gates_ready = sem("gates_ready")
        weights_loaded = sem("weights_loaded")
        x_loaded = [sem(f"x_loaded{i}") for i in range(2)]
        xT_loaded = [sem(f"xT_loaded{i}") for i in range(2)]
        front_steps = sem("front_steps")
        back_steps = sem("back_steps")
        var1_ready = sem("var1_ready")
        scale1_ready = sem("scale1_ready")
        scores_ready = sem("scores_ready")
        scores_free = sem("scores_free")
        negmax_ready = sem("negmax_ready")
        exp_ready = sem("exp_ready")
        expT_ready = sem("expT_ready")
        expT_copied = sem("expT_copied")
        attn_ready = sem("attn_ready")
        attn_used = sem("attn_used")
        x2_stored = [sem(f"x2_stored{i}") for i in range(2)]
        var2_ready = sem("var2_ready")
        rstd2_ready = sem("rstd2_ready")
        bias2_ready = sem("bias2_ready")
        rows_normed = sem("rows_normed")
        gap_ready = sem("gap_ready")
        gap_exp_ready = sem("gap_exp_ready")
        picks_ready = sem("picks_ready")
        ranks_ready = sem("ranks_ready")
        slots_ready = sem("slots_ready")
        scattered = [sem(f"scattered{i}") for i in range(2)]
        counts_ready = sem("counts_ready")
        table_steps = sem("table_steps")
        tables_ready = sem("tables_ready")
        pads_written = sem("pads_written")
        tile_loaded = [sem(f"tile_loaded{i}") for i in range(XR)]
        tileT_ready = sem("tileT_ready")
        tileT_copied = sem("tileT_copied")
        gate_ready = sem("gate_ready")
        silu_ready = sem("silu_ready")
        up_ready = sem("up_ready")
        hidden_ready = sem("hidden_ready")
        hiddenT_ready = sem("hiddenT_ready")
        hiddenT_copied = sem("hiddenT_copied")
        down_ready = sem("down_ready")
        y_ready = sem("y_ready")
        y_added = sem("y_added")
        sp_passed = sem("sp_passed")
        pool_passed = sem("pool_passed")
        dve_passed = sem("dve_passed")

        SCORES_FREE0 = 2
        EXPT_COPIED0 = 1
        ATTN_USED0 = 1
        SCATTERED0 = 16 * TOPK * G
        Y_READY0 = 2
        Y_ADDED0 = 16 * 2
        FRONT, BACK = 4, 18
        SMALL = 16 * (BATCH + 9)

        def walk(eng, front, back):
            front(0, 0, 0)
            with eng.Fori(0, HALF - 1) as i:
                front(2 * i + 1, 1, i)
                back(2 * i, 0, i)
                front(2 * i + 2, 0, i + 1)
                back(2 * i + 1, 1, i)
            front(GROUPS - 1, 1, HALF - 1)
            back(GROUPS - 2, 0, HALF - 1)
            back(GROUPS - 1, 1, HALF - 1)

        block = es.enter_context(nc.Block())

        @block.sync
        def _(sp):
            x_v = x.rearrange("(n p) d -> p n d", p=P)
            out_v = out[0:N, :].rearrange("(n p) d -> p n d", p=P)
            xT_v = xT.rearrange("(c p) n -> p c n", p=P)

            def load_x(g, r):
                sp.dma_start(xg[:, r], x_v[:, bass.ds(g * G, G), :]).then_inc(x_loaded[r], 16)
                sp.dma_start(xTg[:, r], xT_v[:, :, bass.ds(g * (G * P), G * P)]).then_inc(xT_loaded[r], 16)

            def small(dst, src):
                sp.dma_start(dst, src).then_inc(small_loaded, 16)

            sp.wait_ge(kr_zeroed, 1)
            small(kr[0:CTX, :, :], ctx_rows.rearrange("b k d -> k b d"))
            for b in range(BATCH):
                small(kr[CTX:CTX + NE, b, :], router)
            small(ctxT_sb[:], ctxT.rearrange("(c p) k -> p c k", p=P))
            small(w_sb[:], w_rows.rearrange("(c p) d -> p c d", p=P))
            small(wT_sb[:, :, 0:D], wT.rearrange("(c p) d -> p c d", p=P))
            small(brow[0:1, 0:D], b_row)
            small(bcol[:], b_col)
            small(lens_i[:], lens.to_broadcast([P, BATCH]))
            small(graw[:, 0:1], g_x.to_broadcast([P, 1]))
            small(graw[:, 1:2], g_f.to_broadcast([P, 1]))
            load_x(0, 0)
            load_x(1, 1)
            for e in range(NE):
                for k, w in ((0, w_gateT), (1, w_upT)):
                    sp.dma_start(WGU[:, e * GUW:(e + 1) * GUW].rearrange("p (c k h) -> p c k h", c=DC, k=2)[:, :, k, :],
                                 w[e].rearrange("(c p) h -> p c h", p=P)).then_inc(weights_loaded, 16)
                sp.dma_start(WD[:, e * DW:(e + 1) * DW].rearrange("p (c d) -> p c d", c=HC),
                             w_downT[e].rearrange("(c p) d -> p c d", p=P)).then_inc(weights_loaded, 16)

            def turn(g, r, i):
                sp.wait_ge(attn_used, g + 1 + ATTN_USED0)
                sp.dma_start(out_v[:, bass.ds(g * G, G), :], xg[:, r]).then_inc(x2_stored[r], 16)

            def refill(g, r, i):
                sp.wait_ge(x2_stored[r], 16 * (i + 1))
                sp.sem_inc(sp_passed)
                sp.wait_ge(rows_normed, g + 1)
                load_x(g + 2, r)

            with sp.Fori(0, HALF - 1) as i:
                turn(2 * i, 0, i)
                refill(2 * i, 0, i)
                turn(2 * i + 1, 1, i)
                refill(2 * i + 1, 1, i)
            turn(GROUPS - 2, 0, HALF - 1)
            turn(GROUPS - 1, 1, HALF - 1)

            sp.wait_ge(tables_ready, 1)
            for e in range(NE):
                at = sp.value_load(pad_row[0:1, e:e + 1], min_val=0, max_val=NE * REGION - P)
                sp.dma_start(sorted_rows[bass.ds(at, P), :], pad_tile[:]).then_inc(pads_written, 16)
            sp.wait_ge(pads_written, 16 * NE)
            sp.wait_ge(y_added, Y_ADDED0)
            for r in range(2):
                sp.wait_ge(scattered[r], SCATTERED0 + 16 * TOPK * G * HALF)
                sp.wait_ge(x2_stored[r], 16 * HALF)

            def load_tile(j, s):
                at = sp.value_load(tile_row[0:1, bass.ds(j, 1)], min_val=0,
                                   max_val=NE * REGION + (SPARE - 1) * P)
                sp.dma_start(xt[:, s], sorted_rows[bass.ds(at, P), :]).then_inc(tile_loaded[s], 16)

            for s in range(XR):
                load_tile(s, s)
            with sp.Fori(1, TILES // XR) as i:
                for s in range(XR):
                    sp.wait_ge(y_added, 16 * (XR * i + s - XR + 1) + Y_ADDED0)
                    load_tile(XR * i + s, s)
            for j in range(TILES // XR * XR, TILES):
                sp.wait_ge(y_added, 16 * (j - XR + 1) + Y_ADDED0)
                load_tile(j, j % XR)
            sp.wait_ge(y_added, 16 * TILES + Y_ADDED0)

        @block.gpsimd
        def _(pool):
            nc.gpsimd.memset(ident[:], 1.0)
            nc.gpsimd.memset(tri[:], 1.0)
            nc.gpsimd.memset(ones[:], 1.0)
            nc.gpsimd.memset(pad_tile[:], 0.0)
            nc.gpsimd.memset(one8[:], 1.0)
            nc.gpsimd.memset(minus_half[:], -0.5).then_inc(pool_consts, 1)
            pool.wait_ge(pool_consts, 1)
            nc.gpsimd.affine_select(out=ident[:], in_=ident[:], pattern=[[-1, P]], compare_op=ALU.is_equal,
                                    fill=0.0, base=0, channel_multiplier=1)
            nc.gpsimd.affine_select(out=tri[:], in_=tri[:], pattern=[[1, P]], compare_op=ALU.is_gt,
                                    fill=0.0, base=0, channel_multiplier=-1)
            for ramp, step, count, by_partition in ((kpos, 1, CTX, 0), (qpos, P, QT, 1), (iota_e, 1, NE, 0),
                                                    (region, REGION, NE, 0), (J, 1, TILES, 0), (tok, P, NT, 1)):
                nc.gpsimd.iota(ramp[:], [[step, count]], base=0, channel_multiplier=by_partition,
                               allow_small_or_imprecise_dtypes=True).then_inc(pool_consts, 1)
            nc.gpsimd.iota(pad_tile[:, TOK:TOK + 1].bitcast(I32), [[1, 1]], base=N,
                           channel_multiplier=1).then_inc(pads_ready, 1)
            pool.wait_ge(pads_ready, 1)
            spare = sorted_rows[NE * REGION:, :].rearrange("(k p) c -> p k c", p=P)
            for r, tiles in enumerate(((0, SPARE // 2), (SPARE // 2, SPARE))):
                count = tiles[1] - tiles[0]
                nc.gpsimd.dma_start(spare[:, tiles[0]:tiles[1], :],
                                    pad_tile[:].unsqueeze(1).to_broadcast([P, count, ROW])
                                    ).then_inc(scattered[r], SCATTERED0)
            nc.gpsimd.dma_start(out[N:N + P, :], pad_tile[:, 0:D]).then_inc(y_added, Y_ADDED0)

            def front(g, r, i):
                pool.wait_ge(var1_ready, g + 1)
                nc.gpsimd.tensor_tensor(out=sc1[:, r], in0=ve1[:, r], in1=minus_half[:],
                                        op=ALU.pow).then_inc(scale1_ready, 1)

            def back(g, r, i):
                pool.wait_ge(var2_ready, g + 1)
                nc.gpsimd.tensor_tensor(out=rstd2[:], in0=ve2[:], in1=minus_half[:],
                                        op=ALU.pow).then_inc(rstd2_ready, 1)
                pool.wait_ge(slots_ready, g + 1)
                pool.wait_ge(rows_normed, g + 1)
                pool.sem_inc(pool_passed)
                for t in range(G):
                    for k in range(TOPK):
                        nc.gpsimd.indirect_dma_start(
                            out=sorted_rows,
                            out_offset=bass.IndirectOffsetOnAxis(ap=slot[:, r, k, t:t + 1], axis=0),
                            in_=pay[:, r, t, :], in_offset=None).then_inc(scattered[r], 16)

            walk(pool, front, back)

            def add(j, s):
                pool.wait_ge(y_ready, j + 1 + Y_READY0)
                pool.wait_ge(y_added, 16 * j + Y_ADDED0)
                pool.sem_inc(pool_passed)
                nc.gpsimd.indirect_dma_start(
                    out=out, out_offset=bass.IndirectOffsetOnAxis(ap=xt[:, s, TOK:TOK + 1].bitcast(I32), axis=0),
                    in_=y[:, s % 2, :], in_offset=None, compute_op=ALU.add).then_inc(y_added, 16)

            with pool.Fori(0, TILES // XR) as i:
                for s in range(XR):
                    add(XR * i + s, s)
            for j in range(TILES // XR * XR, TILES):
                add(j, j % XR)

        @block.scalar
        def _(act):
            act.sem_inc(expT_copied, EXPT_COPIED0)
            act.sem_inc(y_ready, Y_READY0)
            act.wait_ge(small_loaded, SMALL)
            nc.scalar.activation(gates[:], graw[:], ACT.Tanh).then_inc(gates_ready, 1)
            for b in range(BATCH):
                act.wait_ge(krT_ready, b + 1)
                nc.scalar.copy(krT[:, b], O[:, b, 0:DC * KR].rearrange("p (c k) -> p c k", c=DC)).then_inc(krT_copied, 1)
            act.wait_ge(wr_ready, 1)
            nc.scalar.copy(brow[0:1, D:OW], R[0:1, 0:NE])
            nc.scalar.copy(wT_sb[:, :, D:OW], S[:, 0, 0:DC * NE].rearrange("p (c k) -> p c k", c=DC)).then_inc(wr_copied, 1)
            for b in range(BATCH):
                act.wait_ge(vw_ready, b + 1)
                nc.scalar.copy(vw[:, b], O[0:CTX, b, 0:OW]).then_inc(vw_copied, 1)

            def front(g, r, i):
                act.wait_ge(negmax_ready, g + 1)
                for t in range(G):
                    last = nc.scalar.activation(ex[:, r, t], sm[:, r, t], ACT.Exp, bias=nb[:, r, t:t + 1],
                                                scale=sc1[:, r, t:t + 1], accum_out=rs[:, r, t:t + 1])
                last.then_inc(exp_ready, 1)

            def back(g, r, i):
                act.wait_ge(expT_ready, g + 1)
                nc.scalar.copy(eT[:], ET[0:CTX, :]).then_inc(expT_copied, 1)
                act.wait_ge(gap_ready, g + 1)
                nc.scalar.activation(ed[:], dl[:], ACT.Exp).then_inc(gap_exp_ready, 1)
                act.wait_ge(bias2_ready, g + 1)
                act.wait_ge(scattered[r], 16 * TOPK * G * i + SCATTERED0)
                for t in range(G):
                    nc.scalar.activation(pay[:, r, t, 0:D], xg[:, r, t], ACT.Identity,
                                         bias=nmr2[:, t:t + 1], scale=rstd2[:, t:t + 1])
                nc.scalar.copy(pay[:, r, :, TOK].bitcast(I32), tok[:, bass.ds(g * G, G)]).then_inc(rows_normed, 1)

            walk(act, front, back)

            def copy_tileT(j, s):
                act.wait_ge(tileT_ready, j + 1)
                nc.scalar.copy(xtT[:, s % 2], XT[:, s % 2, 0:D]).then_inc(tileT_copied, 1)

            def silu(j, s):
                act.wait_ge(gate_ready, j + 1)
                nc.scalar.activation(hid[:, s % 2], GT[:], ACT.Silu).then_inc(silu_ready, 1)

            def copy_hiddenT(j):
                act.wait_ge(hiddenT_ready, j + 1)
                nc.scalar.copy(hT[:], HT[:]).then_inc(hiddenT_copied, 1)

            def weigh(j, s):
                e = act.value_load(tile_expert[0:1, bass.ds(j, 1)], min_val=0, max_val=NE - 1)
                act.wait_ge(down_ready, j + 1)
                act.wait_ge(y_added, 16 * (j - 1) + Y_ADDED0)
                nc.scalar.mul(y[:, s % 2], Y[:, s % 2, 0:D], xt[:, s, bass.ds(e + CW, 1)]).then_inc(y_ready, 1)

            def turn(j, s, after=2):
                if after > 0:
                    silu(j + 1, s + 1)
                copy_hiddenT(j)
                if after > 1:
                    copy_tileT(j + 2, s + 2)
                weigh(j, s)

            act.wait_ge(tables_ready, 1)
            copy_tileT(0, 0)
            copy_tileT(1, 1)
            silu(0, 0)
            with act.Fori(0, TURNS) as i:
                for s in range(XR):
                    turn(XR * i + s, s)
            for j in range(TURNS * XR, TILES):
                turn(j, j % XR, TILES - 1 - j)

        @block.vector
        def _(dve):
            def per_expert(v):
                return v.unsqueeze(2).to_broadcast([P, G, NE])

            def per_tile(v):
                return v.unsqueeze(1).to_broadcast([P, G, NE])

            dve.sem_inc(scores_free, SCORES_FREE0)
            dve.sem_inc(attn_used, ATTN_USED0)
            nc.vector.memset(carry[:], 0.0)
            nc.vector.memset(ones_row[:], 1.0)
            nc.vector.memset(kr[:], 0.0).then_inc(kr_zeroed, 1)
            dve.wait_ge(small_loaded, SMALL)
            for b in range(BATCH):
                last = nc.vector.bn_stats(kst[:, b], kr[:, b])
            last.then_inc(setup_steps, 1)
            dve.wait_ge(setup_steps, 1)
            for b in range(BATCH):
                last = nc.vector.bn_aggr(kmv[:, b], kst[:, b])
            last.then_inc(setup_steps, 1)
            dve.wait_ge(setup_steps, 2)
            for b in range(BATCH):
                nc.vector.tensor_scalar(kr[:, b], kr[:, b], kmv[:, b, 0:1], None,
                                        ALU.subtract).then_inc(keys_centred, 1)
            nc.vector.tensor_copy(lens_f[:], lens_i[:]).then_inc(setup_steps, 1)
            dve.wait_ge(setup_steps, 3)
            dve.wait_ge(pool_consts, 7)
            for b in range(BATCH):
                nc.vector.tensor_scalar(kmask[:, b * CTX:(b + 1) * CTX], kpos[:], lens_f[:, b:b + 1], MASKED,
                                        ALU.is_ge, ALU.mult)
                last = nc.vector.tensor_scalar(qmask[:, b * QT:(b + 1) * QT], qpos[:],
                                               lens_f[:, b:b + 1], None, ALU.is_ge)
            last.then_inc(setup_steps, 1)
            dve.wait_ge(setup_steps, 4)
            dve.wait_ge(gates_ready, 1)

            def front(g, r, i):
                count = [0]

                def step(ins):
                    count[0] += 1
                    ins.then_inc(front_steps, 1)
                    dve.wait_ge(front_steps, g * FRONT + count[0])
                    if count[0] == 1:
                        dve.sem_inc(dve_passed)

                dve.wait_ge(x_loaded[r], 16 * i + 16)
                for t in range(G):
                    last = nc.vector.bn_stats(st1[:, t], xg[:, r, t])
                step(last)
                for t in range(G):
                    last = nc.vector.bn_aggr(mv1[:, t], st1[:, t])
                step(last)
                nc.vector.tensor_scalar(ve1[:, r], mv1[:, :, 1], EPS, float(D), ALU.add,
                                        ALU.mult).then_inc(var1_ready, 1)
                dve.wait_ge(scores_ready, g + 1)
                for t in range(G):
                    last = nc.vector.scalar_tensor_tensor(
                        out=sm[:, r, t], in0=kmask[:, bass.ds(i * CTX, CTX)],
                        scalar=qmask[:, bass.ds(g * G + t, 1)],
                        in1=S[:, r, t * KR:t * KR + CTX], op0=ALU.mult, op1=ALU.add)
                step(last)
                nc.vector.tensor_copy(
                    sr[:, r], S[:, r, 0:G * KR].rearrange("p (t k) -> p t k", t=G)[:, :, CTX:CTX + NE]
                ).then_inc(scores_free, 1)
                step(nc.vector.tensor_reduce(mx[:], sm[:, r], axis=AX.X, op=ALU.max))
                dve.wait_ge(scale1_ready, g + 1)
                nc.vector.scalar_tensor_tensor(out=nb[:, r], in0=mx[:], scalar=-1.0, in1=sc1[:, r],
                                               op0=ALU.mult, op1=ALU.mult).then_inc(negmax_ready, 1)
                assert count[0] == FRONT

            def back(g, r, i):
                count = [0]

                def step(ins):
                    count[0] += 1
                    ins.then_inc(back_steps, 1)
                    dve.wait_ge(back_steps, g * BACK + count[0])
                    if count[0] in (3, 6):
                        dve.sem_inc(dve_passed)

                dve.wait_ge(exp_ready, g + 1)
                step(nc.vector.reciprocal(rg[:], rs[:, r]))
                step(nc.vector.tensor_scalar(rgt[:], rg[:], gates[:, 0:1], None, ALU.mult))
                dve.wait_ge(attn_ready, g + 1)
                nc.vector.tensor_tensor(out=lg0[:], in0=O[:, :, D:OW], in1=per_expert(rgt[:]), op=ALU.mult)
                for t in range(G):
                    last = nc.vector.scalar_tensor_tensor(out=xg[:, r, t], in0=O[:, t, 0:D], scalar=rgt[:, t:t + 1],
                                                          in1=xg[:, r, t], op0=ALU.mult, op1=ALU.add)
                last.then_inc(attn_used, 1)
                dve.wait_ge(attn_used, g + 1 + ATTN_USED0)
                for t in range(G):
                    last = nc.vector.bn_stats(st2[:, t], xg[:, r, t])
                step(last)
                for t in range(G):
                    last = nc.vector.bn_aggr(mv2[:, t], st2[:, t])
                step(last)
                nc.vector.tensor_scalar(ve2[:], mv2[:, :, 1], EPS, None, ALU.add).then_inc(var2_ready, 1)
                step(nc.vector.tensor_tensor(out=lg1[:], in0=lg0[:], in1=sr[:, r], op=ALU.add))
                dve.wait_ge(rstd2_ready, g + 1)
                nc.vector.scalar_tensor_tensor(out=nmr2[:], in0=mv2[:, :, 0], scalar=-1.0, in1=rstd2[:],
                                               op0=ALU.mult, op1=ALU.mult).then_inc(bias2_ready, 1)
                step(nc.vector.tensor_tensor(out=lg[:], in0=lg1[:], in1=per_expert(rstd2[:]), op=ALU.mult))
                for t in range(G):
                    last = nc.vector.max(m8[:, t], lg[:, t])
                step(last)
                nc.vector.tensor_tensor(out=dl[:], in0=m8[:, :, 1], in1=m8[:, :, 0],
                                        op=ALU.subtract).then_inc(gap_ready, 1)
                for t in range(G):
                    last = nc.vector.max_index(mi[:, t], m8[:, t], lg[:, t])
                step(last)
                for k in range(TOPK):
                    last = nc.vector.tensor_tensor(out=oh[:, k], in0=per_tile(iota_e[:]),
                                                   in1=per_expert(mi[:, :, k]), op=ALU.is_equal)
                step(last)
                nc.vector.tensor_tensor(out=picks[:], in0=oh[:, 0], in1=oh[:, 1],
                                        op=ALU.add).then_inc(picks_ready, 1)
                dve.wait_ge(gap_exp_ready, g + 1)
                step(nc.vector.tensor_scalar(ed1[:], ed[:], 1.0, None, ALU.add))
                step(nc.vector.reciprocal(rw[:], ed1[:]))
                step(nc.vector.tensor_scalar(wk[:, 0], rw[:], gates[:, 1:2], None, ALU.mult))
                step(nc.vector.tensor_tensor(out=wk[:, 1], in0=wk[:, 0], in1=ed[:], op=ALU.mult))
                for k in range(TOPK):
                    last = nc.vector.tensor_tensor(out=cw[:, k], in0=oh[:, k], in1=per_expert(wk[:, k]), op=ALU.mult)
                step(last)
                dve.wait_ge(scattered[r], 16 * TOPK * G * i + SCATTERED0)
                nc.vector.tensor_tensor(out=pay[:, r, :, CW:ROW], in0=cw[:, 0], in1=cw[:, 1], op=ALU.add)
                step(nc.vector.tensor_reduce(npicks[:], picks[:].rearrange("p t e -> p e t"), axis=AX.X, op=ALU.add))
                dve.wait_ge(ranks_ready, g + 1)
                step(nc.vector.tensor_tensor(out=place[:], in0=R[:, 0:G * NE].rearrange("p (t e) -> p t e", t=G),
                                             in1=per_tile(region[:]), op=ALU.add))
                step(nc.vector.tensor_tensor(out=carry[:], in0=carry[:], in1=npicks[:], op=ALU.add))
                for k in range(TOPK):
                    last = nc.vector.tensor_tensor(out=po[:, k], in0=oh[:, k], in1=place[:], op=ALU.mult)
                step(last)
                with nc.allow_low_precision(reason="whole numbers below 2**24, summed in float32"):
                    nc.vector.tensor_reduce(slot[:, r], po[:], axis=AX.X, op=ALU.add).then_inc(slots_ready, 1)
                assert count[0] == BACK, count

            walk(dve, front, back)

            done = [0]

            def step(ins):
                done[0] += 1
                ins.then_inc(table_steps, 1)
                dve.wait_ge(table_steps, done[0])

            dve.wait_ge(counts_ready, 1)
            nc.vector.tensor_copy(cnt[:], R[0:1, 0:NE])
            step(nc.vector.tensor_scalar(nti[:], R[0:1, 0:NE], float(P - 1), None, ALU.add))
            nc.vector.tensor_tensor(out=pad_row[:], in0=region[0:1, :], in1=cnt[:], op=ALU.add)
            step(nc.vector.tensor_single_scalar(nts[:], nti[:], P.bit_length() - 1, ALU.logical_shift_right))
            step(nc.vector.tensor_copy(ntf[:], nts[:]))
            step(nc.vector.tensor_tensor_scan(cum[:], one8[:], ntf[:], 0.0, ALU.mult, ALU.add))
            step(nc.vector.tensor_tensor(out=past[:], in0=J[:].unsqueeze(2).to_broadcast([1, TILES, NE]),
                                         in1=cum[:].unsqueeze(1).to_broadcast([1, TILES, NE]), op=ALU.is_ge))
            nc.vector.tensor_reduce(tex[:], past[:], axis=AX.X, op=ALU.add)
            step(nc.vector.tensor_tensor(out=pastn[:], in0=past[:],
                                         in1=ntf[:].unsqueeze(1).to_broadcast([1, TILES, NE]), op=ALU.mult))
            step(nc.vector.tensor_reduce(before[:], pastn[:], axis=AX.X, op=ALU.add))
            step(nc.vector.tensor_tensor(out=rel[:], in0=J[:], in1=before[:], op=ALU.subtract))
            step(nc.vector.tensor_scalar(rel128[:], rel[:], float(P), None, ALU.mult))
            nc.vector.tensor_scalar(tile_expert[:], tex[:], float(NE - 1), None, ALU.min)
            nc.vector.scalar_tensor_tensor(out=tile_row[:], in0=tex[:], scalar=float(REGION), in1=rel128[:],
                                           op0=ALU.mult, op1=ALU.add).then_inc(tables_ready, 1)

            def gate_up(j, s):
                dve.wait_ge(silu_ready, j + 1)
                dve.wait_ge(up_ready, j + 1)
                nc.vector.tensor_tensor(out=hid[:, s % 2], in0=hid[:, s % 2], in1=UP[:],
                                        op=ALU.mult).then_inc(hidden_ready, 1)

            with dve.Fori(0, TURNS) as i:
                for s in range(XR):
                    gate_up(XR * i + s, s)
            for j in range(TURNS * XR, TILES):
                gate_up(j, j % XR)

        @block.tensor
        def _(pe):
            mm = nc.tensor.matmul
            pe.wait_ge(pool_consts, 2)
            for b in range(BATCH):
                pe.wait_ge(keys_centred, b + 1)
                for c in range(DC):
                    last = nc.tensor.transpose(O[:, b, c * KR:(c + 1) * KR], kr[:, b, c * P:(c + 1) * P],
                                               ident[0:KR, 0:KR])
                last.then_inc(krT_ready, 1)
            pe.wait_ge(krT_copied, BATCH)
            pe.wait_ge(small_loaded, SMALL)
            routerT = krT[:, 0, :, CTX:CTX + NE]
            for dc in range(DC):
                for c in range(DC):
                    mm(S[:, 0, dc * NE:(dc + 1) * NE], w_sb[:, c, dc * P:(dc + 1) * P], routerT[:, c],
                       start=(c == 0), stop=(c == DC - 1))
            for c in range(DC):
                last = mm(R[0:1, 0:NE], bcol[:, c:c + 1], routerT[:, c], start=(c == 0), stop=(c == DC - 1))
            last.then_inc(wr_ready, 1)
            pe.wait_ge(wr_copied, 1)
            for b in range(BATCH):
                for c in range(DC):
                    mm(O[0:CTX, b, 0:OW], ctxT_sb[:, c, b * CTX:(b + 1) * CTX], wT_sb[:, c], start=(c == 0), stop=False)
                mm(O[0:CTX, b, 0:OW], ones_row[:], brow[:], start=False, stop=True).then_inc(vw_ready, 1)
            pe.wait_ge(vw_copied, BATCH)

            def front(g, r, i):
                pe.wait_ge(xT_loaded[r], 16 * i + 16)
                pe.wait_ge(scores_free, g + 1)
                for t in range(G):
                    for c in range(DC):
                        last = mm(S[:, r, t * KR:(t + 1) * KR], xTg[:, r, c, t * P:(t + 1) * P],
                                  krT[:, bass.ds(i, 1), c, :].rearrange("p b k -> p (b k)"),
                                  start=(c == 0), stop=(c == DC - 1))
                last.then_inc(scores_ready, 1)

            def back(g, r, i):
                pe.wait_ge(exp_ready, g + 1)
                pe.wait_ge(expT_copied, g + EXPT_COPIED0)
                for t in range(G):
                    last = nc.tensor.transpose(ET[0:CTX, t * P:(t + 1) * P], ex[:, r, t], ident[:])
                last.then_inc(expT_ready, 1)
                pe.wait_ge(expT_copied, g + 1 + EXPT_COPIED0)
                pe.wait_ge(attn_used, g + ATTN_USED0)
                for t in range(G):
                    last = mm(O[:, t, 0:OW], eT[:, t * P:(t + 1) * P],
                              vw[:, bass.ds(i, 1), :].rearrange("p b k -> p (b k)"), start=True, stop=True)
                last.then_inc(attn_ready, 1)
                pe.wait_ge(picks_ready, g + 1)
                ranks = R[:, 0:G * NE].rearrange("p (t e) -> p t e", t=G)
                mm(ranks, ones[:], carry[:].unsqueeze(1).to_broadcast([P, G, NE]), start=True, stop=False)
                for t in range(G - 1):
                    mm(ranks[:, t + 1:G], ones[:], picks[:, t:t + 1].to_broadcast([P, G - 1 - t, NE]),
                       start=False, stop=False, skip_group_check=True)
                mm(ranks, tri[:], picks[:], start=False, stop=True).then_inc(ranks_ready, 1)

            walk(pe, front, back)

            pe.wait_ge(back_steps, GROUPS * BACK)
            mm(R[:, 0:NE], ones[:], carry[:], start=True, stop=True).then_inc(counts_ready, 1)

            def expert(j):
                return pe.value_load(tile_expert[0:1, bass.ds(j, 1)], min_val=0, max_val=NE - 1)

            def transpose_tile(s):
                for c in range(DC):
                    last = nc.tensor.transpose(XT[:, s % 2, c * P:(c + 1) * P], xt[:, s % XR, c * P:(c + 1) * P], ident[:])
                last.then_inc(tileT_ready, 1)

            def first_layer(bank, s, e, k):
                for c in range(DC):
                    last = mm(bank[:], xtT[:, s % 2, c * P:(c + 1) * P],
                              WGU[:, bass.ds(e * GUW + (c * 2 + k) * HID, HID)], start=(c == 0), stop=(c == DC - 1))
                return last

            def gate(j, s, e):
                pe.wait_ge(tileT_copied, j + 1)
                if not isinstance(j, int) or j > 0:
                    pe.wait_ge(silu_ready, j)
                first_layer(GT, s, e, 0).then_inc(gate_ready, 1)

            def up(j, s, e):
                if not isinstance(j, int) or j > 0:
                    pe.wait_ge(hidden_ready, j)
                first_layer(UP, s, e, 1).then_inc(up_ready, 1)

            def transpose_hidden(j, s):
                pe.wait_ge(hidden_ready, j + 1)
                for c in range(HC):
                    last = nc.tensor.transpose(HT[:, c * P:(c + 1) * P], hid[:, s % 2, c * P:(c + 1) * P], ident[:])
                last.then_inc(hiddenT_ready, 1)

            def down(j, s, e):
                pe.wait_ge(hiddenT_copied, j + 1)
                pe.wait_ge(y_ready, j - 1 + Y_READY0)
                for c in range(HC):
                    last = mm(Y[:, s % 2, 0:D], hT[:, c * P:(c + 1) * P], WD[:, bass.ds(e * DW + c * D, D)],
                              start=(c == 0), stop=(c == HC - 1))
                last.then_inc(down_ready, 1)

            def turn(j, s, turns, after=2):
                e, e1 = expert(j), expert(j + 1) if after > 0 else None
                if after > 0:
                    gate(j + 1, s + 1, e1)
                transpose_hidden(j, s)
                if after > 0:
                    up(j + 1, s + 1, e1)
                if after > 1:
                    pe.wait_ge(tile_loaded[(s + 2) % XR], 16 * (turns + 1 + (s + 2) // XR))
                    pe.wait_ge(tileT_copied, j + 1)
                    transpose_tile(s + 2)
                down(j, s, e)

            pe.wait_ge(tables_ready, 1)
            pe.wait_ge(weights_loaded, 16 * 3 * NE)
            e0 = expert(0)
            for j in range(2):
                pe.wait_ge(tile_loaded[j], 16)
                transpose_tile(j)
            gate(0, 0, e0)
            up(0, 0, e0)
            with pe.Fori(0, TURNS) as i:
                for s in range(XR):
                    turn(XR * i + s, s, i)
            for j in range(TURNS * XR, TILES):
                turn(j, j % XR, TURNS, TILES - 1 - j)


def kernel(x, ctx_1024, _lenS2, g_xattn, g_ffn, L0_xattn_W, L0_xattn_b, L0_ffn_router_w, L0_ffn_w_gate,
           L0_ffn_w_up, L0_ffn_w_down):
    import numpy as np
    import concourse.bacc as bacc
    from concourse.bass_utils import run_bass_kernel_spmd

    rows = np.asarray(x).reshape(N, D)
    ctx = np.asarray(ctx_1024)
    W = np.asarray(L0_xattn_W)
    b = np.asarray(L0_xattn_b)
    laid_out = {
        "x": rows, "xT": rows.T,
        "ctx_rows": ctx, "ctxT": ctx.reshape(BATCH * CTX, D).T,
        "lens": np.asarray(_lenS2).reshape(1, BATCH),
        "g_x": np.asarray(g_xattn).reshape(1, 1), "g_f": np.asarray(g_ffn).reshape(1, 1),
        "w_rows": W, "wT": W.T, "b_row": b.reshape(1, D), "b_col": b.reshape(DC, P).T,
        "router": np.asarray(L0_ffn_router_w),
        "w_gateT": np.asarray(L0_ffn_w_gate).transpose(0, 2, 1),
        "w_upT": np.asarray(L0_ffn_w_up).transpose(0, 2, 1),
        "w_downT": np.asarray(L0_ffn_w_down).transpose(0, 2, 1),
    }
    nc = bacc.Bacc("TRN2", target_bir_lowering=False, num_devices=1, dynamic_dma_scratch_size=8192)
    arrays, args = {}, []
    for name, a in laid_out.items():
        a = np.ascontiguousarray(a)
        arrays[f"in_{name}"] = a
        args.append(nc.dram_tensor(f"in_{name}", a.shape, mybir.dt.from_np(a.dtype), kind="ExternalInput").ap())
    args.append(nc.dram_tensor("out_rows", (N + P, D), F32, kind="ExternalOutput").ap())
    moe_flamingo(nc, *args)
    r = run_bass_kernel_spmd(nc, [arrays], core_ids=[0])
    return r.results[0]["out_rows"][:N].reshape(BATCH, SEQ, D)
```

```python
import concourse.bass as bass
from concourse import mybir
from contextlib import ExitStack

F32 = mybir.dt.float32
F32R = mybir.dt.float32r
BF16 = mybir.dt.bfloat16
I32 = mybir.dt.int32
U32 = mybir.dt.uint32
ALU = mybir.AluOpType
ACT = mybir.ActivationFunctionType
AX = mybir.AxisListType

P = 128
BATCH, SEQ, D = 4, 1024, 256
CTX = 77
NE, HID, TOPK = 8, 512, 2
N = BATCH * SEQ
DC, HC = D // P, HID // P
G = 4
GROUPS = N // (G * P)
HALF = GROUPS // 2
NT = N // P
QT = SEQ // P
KR = 96
OW = D + NE
EPS = 1e-5
MASKED = -float(2 ** 100)

REGION = N + P
TILES = (TOPK * N - NE) // P + NE
SPARE = TILES - TOPK * N // P
ROW = D + 1 + NE
TOK, CW = D, D + 1
XR = 8
TURNS = (TILES - 2) // XR
DOWN = 2 * HID
HALVES, HW = DC, DOWN + HC // DC * D
CUTS = 4
PIECE = HALVES * HW // CUTS
EARLY = 6


def moe_flamingo(nc, x, xT, ctx_rows, ctxT, lens, g_x, g_f, w_rows, wT, b_row, b_col, router, weights, out):
    sorted_rows = nc.dram_tensor("sorted_rows", (NE * REGION + SPARE * P, ROW), F32, kind="Internal").ap()
    es = ExitStack()
    with es:
        def sb(name, shape, dt=F32, stack=es):
            return stack.enter_context(nc.sbuf_tensor(name, shape, dt))

        def pb(name, shape, stack):
            return stack.enter_context(nc.psum_tensor(name, shape, F32))

        def sem(name):
            return es.enter_context(nc.semaphore(name))

        ident = sb("ident", [P, P])
        gates = sb("gates", [P, 2])
        tile_expert = sb("tile_expert", [1, TILES], I32)
        tile_row = sb("tile_row", [1, TILES], I32)
        pad_row = sb("pad_row", [1, NE], I32)
        skewed = sb("skewed", [1, 1], I32)
        pad_tile = sb("pad_tile", [P, ROW])

        lo = ExitStack()
        raw = [sb(f"raw{h}", [P, NE, HW], F32, lo) for h in range(HALVES)]
        lo.close()
        w_low = [sb(f"w_low{h}", [P, NE * HW], F32R) for h in range(HALVES)]
        w_high0 = sb("w_high0", [P, NE * HW], F32R)

        a = ExitStack()
        ctxT_sb = sb("ctxT_sb", [P, DC, BATCH * CTX], F32, a)
        w_sb = sb("w_sb", [P, DC, D], F32, a)
        wT_sb = sb("wT_sb", [P, DC, OW], F32, a)
        xg = sb("xg", [P, 4 * G, D], F32, a)
        xTg = sb("xTg", [P, 2, DC, G * P], F32, a)
        pay = sb("pay", [P, 2, G, ROW], F32, a)
        kr = sb("kr", [KR, BATCH, D], F32, a)
        krT = sb("krT", [P, BATCH, DC, KR], F32, a)
        brow = sb("brow", [1, OW], F32, a)
        bcol = sb("bcol", [P, DC], F32, a)
        ones_row = sb("ones_row", [1, CTX], F32, a)
        vw = sb("vw", [CTX, BATCH, OW], F32, a)
        kst = sb("kst", [KR, BATCH, 6], F32, a)
        kmv = sb("kmv", [KR, BATCH, 2], F32, a)
        lens_i = sb("lens_i", [P, BATCH], I32, a)
        lens_f = sb("lens_f", [P, BATCH], F32, a)
        graw = sb("graw", [P, 2], F32, a)
        kpos = sb("kpos", [P, CTX], F32, a)
        qpos = sb("qpos", [P, QT], F32, a)
        kmask = sb("kmask", [P, BATCH * CTX], F32, a)
        qmask = sb("qmask", [P, NT], F32, a)
        tri = sb("tri", [P, P], BF16, a)
        ones = sb("ones", [P, P], BF16, a)
        iota_e = sb("iota_e", [P, NE], F32, a)
        region = sb("region", [P, NE], F32, a)
        tok = sb("tok", [P, NT], I32, a)
        st1 = sb("st1", [P, G, 6], F32, a)
        mv1 = sb("mv1", [P, G, 2], F32, a)
        sm = sb("sm", [P, 2, G, CTX], F32, a)
        mx = sb("mx", [P, G], F32, a)
        ve = sb("ve", [P, 2, 2 * G], F32, a)
        lnv = sb("lnv", [P, 2 * G], F32, a)
        rt0 = sb("rt0", [P, 2 * G], F32, a)
        rt0sq = sb("rt0sq", [P, 2 * G], F32, a)
        rt0v = sb("rt0v", [P, 2 * G], F32, a)
        rt0c = sb("rt0c", [P, 2 * G], F32, a)
        rt = sb("rt", [P, 2, 2 * G], F32, a)
        nb = sb("nb", [P, 2, G], F32, a)
        sr = sb("sr", [P, 2, G, NE], F32, a)
        ex = sb("ex", [P, 2, G, CTX], F32, a)
        rs = sb("rs", [P, 2, G], F32, a)
        eT = sb("eT", [CTX, G * P], F32, a)
        rg = sb("rg", [P, G], F32, a)
        rgt = sb("rgt", [P, G], F32, a)
        lg0 = sb("lg0", [P, G, NE], F32, a)
        lg1 = sb("lg1", [P, G, NE], F32, a)
        lg = sb("lg", [P, G, NE], F32, a)
        st2 = sb("st2", [P, G, 6], F32, a)
        mv2 = sb("mv2", [P, G, 2], F32, a)
        rstd2 = sb("rstd2", [P, 2, G], F32, a)
        nmr2 = sb("nmr2", [P, 2, G], F32, a)
        m8 = sb("m8", [P, G, NE], F32, a)
        mi = sb("mi", [P, G, NE], U32, a)
        oh = sb("oh", [P, TOPK, G, NE], F32, a)
        picks = sb("picks", [P, G, NE], BF16, a)
        npicks = sb("npicks", [P, NE], F32, a)
        carry = sb("carry", [P, NE], BF16, a)
        dl = sb("dl", [P, G], F32, a)
        ed = sb("ed", [P, G], F32, a)
        ed1 = sb("ed1", [P, G], F32, a)
        rw = sb("rw", [P, G], F32, a)
        wk = sb("wk", [P, TOPK, G], F32, a)
        cw = sb("cw", [P, TOPK, G, NE], F32, a)
        place = sb("place", [P, G, NE], F32, a)
        po = sb("po", [P, TOPK, G, NE], F32, a)
        slot = sb("slot", [P, 2, TOPK, G], I32, a)
        need = sb("need", [1, NE], F32, a)
        start = sb("start", [1, NE], F32, a)
        skew_f = sb("skew_f", [1, 1], F32, a)
        soon = sb("soon", [1, NE], F32, a)
        J = sb("J", [1, TILES], F32, a)
        cnt = sb("cnt", [1, NE], F32, a)
        nti = sb("nti", [1, NE], I32, a)
        nts = sb("nts", [1, NE], I32, a)
        ntf = sb("ntf", [1, NE], F32, a)
        cum = sb("cum", [1, NE], F32, a)
        one8 = sb("one8", [1, NE], F32, a)
        past = sb("past", [1, TILES, NE], F32, a)
        pastn = sb("pastn", [1, TILES, NE], F32, a)
        tex = sb("tex", [1, TILES], F32, a)
        before = sb("before", [1, TILES], F32, a)
        rel = sb("rel", [1, TILES], F32, a)
        rel128 = sb("rel128", [1, TILES], F32, a)
        S = pb("S", [P, 2, 512], a)
        ET = pb("ET", [P, 512], a)
        R = pb("R", [P, 512], a)
        O = pb("O", [P, G, 512], a)
        a.close()

        w_high = [w_high0, sb("w_high1", [P, NE * HW], F32R)]
        xt = sb("xt", [P, XR, ROW])
        xtT = sb("xtT", [P, 2, 2, D], F32R)
        hid = sb("hid", [P, HID])
        hT = sb("hT", [P, 2, HID], F32R)
        y = sb("y", [P, 2, D])
        XT = pb("XT", [P, 2, 512], es)
        GT = pb("GT", [P, 512], es)
        UP = pb("UP", [P, 512], es)
        HT = pb("HT", [P, 512], es)
        Y = pb("Y", [P, 2, 512], es)

        kr_zeroed = sem("kr_zeroed")
        small_loaded = sem("small_loaded")
        pool_consts = sem("pool_consts")
        pads_ready = sem("pads_ready")
        setup_steps = sem("setup_steps")
        keys_centred = sem("keys_centred")
        krT_ready = sem("krT_ready")
        krT_copied = sem("krT_copied")
        wr_ready = sem("wr_ready")
        wr_copied = sem("wr_copied")
        vw_ready = sem("vw_ready")
        vw_copied = sem("vw_copied")
        gates_ready = sem("gates_ready")
        raw_loaded = sem("raw_loaded")
        raw_late = sem("raw_late")
        dve_steps = sem("dve_steps")
        var_ready = sem("var_ready")
        ln_ready = sem("ln_ready")
        rsqrt_ready = sem("rsqrt_ready")
        scores_ready = sem("scores_ready")
        scores_free = sem("scores_free")
        negmax_ready = sem("negmax_ready")
        exp_ready = sem("exp_ready")
        expT_ready = sem("expT_ready")
        expT_copied = sem("expT_copied")
        attn_ready = sem("attn_ready")
        attn_used = sem("attn_used")
        bias2_ready = sem("bias2_ready")
        rows_normed = sem("rows_normed")
        gap_ready = sem("gap_ready")
        gap_exp_ready = sem("gap_exp_ready")
        picks_ready = sem("picks_ready")
        ranks_ready = sem("ranks_ready")
        slots_ready = sem("slots_ready")
        counts_ready = sem("counts_ready")
        table_steps = sem("table_steps")
        tables_ready = sem("tables_ready")
        pads_written = sem("pads_written")
        tileT_ready = sem("tileT_ready")
        tile_high = sem("tile_high")
        tile_low = sem("tile_low")
        gate_ready = sem("gate_ready")
        silu_ready = sem("silu_ready")
        up_ready = sem("up_ready")
        hidden_ready = sem("hidden_ready")
        hiddenT_ready = sem("hiddenT_ready")
        hidden_high = sem("hidden_high")
        hidden_low = sem("hidden_low")
        down_ready = sem("down_ready")
        y_ready = sem("y_ready")
        y_added = sem("y_added")
        weight_high = sem("weight_high")
        weight_low = sem("weight_low")
        passed_sp = sem("passed_sp")
        passed_pool = sem("passed_pool")
        passed_dve = sem("passed_dve")
        x_loaded = [sem(f"x_loaded{i}") for i in range(2)]
        xT_loaded = [sem(f"xT_loaded{i}") for i in range(2)]
        x2_stored = [sem(f"x2_stored{i}") for i in range(2)]
        scattered = [sem(f"scattered{i}") for i in range(2)]
        tile_loaded = [sem(f"tile_loaded{i}") for i in range(XR)]

        SCATTERED0 = 16 * TOPK * G
        X2_STORED0 = 16
        NORMED0 = 2
        Y_READY0 = 2
        Y_ADDED0 = 16 * 2
        SMALL = 16 * (BATCH + 9)
        STEPS = 26

        def turns(eng, turn):
            with eng.Fori(0, HALF - 1) as i:
                turn(2 * i, 0, i, 2)
                turn(2 * i + 1, 1, i, 2)
            turn(GROUPS - 2, 0, HALF - 1, 1)
            turn(GROUPS - 1, 1, HALF - 1, 0)

        def slot_of(r, i):
            return (i % 2) * (2 * G) + r * G

        block = es.enter_context(nc.Block())

        @block.sync
        def _(sp):
            x_v = x.rearrange("(n p) d -> p n d", p=P)
            out_v = out[0:N, :].rearrange("(n p) d -> p n d", p=P)
            xT_v = xT.rearrange("(c p) n -> p c n", p=P)

            def load_x(g, r, i):
                sp.dma_start(xg[:, bass.ds(slot_of(r, i), G)], x_v[:, bass.ds(g * G, G), :]).then_inc(x_loaded[r], 16)

            def load_xT(g, r):
                sp.dma_start(xTg[:, r], xT_v[:, :, bass.ds(g * (G * P), G * P)]).then_inc(xT_loaded[r], 16)

            def load_weights(e, done):
                for h in range(HALVES):
                    sp.dma_start(raw[h][:, bass.ds(e, 1), :].rearrange("p e n -> p (e n)"),
                                 weights[bass.ds(e, 1), :, h].rearrange("e p n -> p (e n)")).then_inc(done, 16)

            def small(dst, src):
                sp.dma_start(dst, src).then_inc(small_loaded, 16)

            sp.sem_inc(x2_stored[0], X2_STORED0)
            sp.sem_inc(x2_stored[1], X2_STORED0)
            sp.sem_inc(rows_normed, NORMED0)
            sp.wait_ge(kr_zeroed, 1)
            small(kr[0:CTX, :, :], ctx_rows.rearrange("b k d -> k b d"))
            for b in range(BATCH):
                small(kr[CTX:CTX + NE, b, :], router)
            small(graw[:, 0:1], g_x.to_broadcast([P, 1]))
            small(graw[:, 1:2], g_f.to_broadcast([P, 1]))
            small(lens_i[:], lens.to_broadcast([P, BATCH]))
            small(w_sb[:], w_rows.rearrange("(c p) d -> p c d", p=P))
            small(bcol[:], b_col)
            small(ctxT_sb[:], ctxT.rearrange("(c p) k -> p c k", p=P))
            small(wT_sb[:, :, 0:D], wT.rearrange("(c p) d -> p c d", p=P))
            small(brow[0:1, 0:D], b_row)
            for g in range(2):
                load_x(g, g, 0)
                load_xT(g, g)
            def turn(k, r, i, behind):
                if behind > 1:
                    sp.wait_ge(var_ready, k + 1)
                    sp.wait_ge(x2_stored[r], 16 * i + X2_STORED0)
                    sp.wait_ge(rows_normed, k - 1 + NORMED0)
                    load_x(k + 2, r, i + 1)
                    sp.wait_ge(scores_ready, k + 1)
                    sp.sem_inc(passed_sp)
                    load_xT(k + 2, r)
                    load_weights(k, raw_loaded)
                sp.wait_ge(attn_used, k + 1)
                sp.sem_inc(passed_sp)
                sp.dma_start(out_v[:, bass.ds(k * G, G), :], xg[:, bass.ds(slot_of(r, i), G)]).then_inc(x2_stored[r], 16)

            turns(sp, turn)
            for e in range(EARLY, NE):
                load_weights(e, raw_late)

            sp.wait_ge(tables_ready, 1)
            for e in range(NE):
                at = sp.value_load(pad_row[0:1, e:e + 1], min_val=0, max_val=NE * REGION - P)
                sp.dma_start(sorted_rows[bass.ds(at, P), :], pad_tile[:]).then_inc(pads_written, 16)
            sp.wait_ge(pads_written, 16 * NE)
            for r in range(2):
                sp.wait_ge(scattered[r], SCATTERED0 + 16 * TOPK * G * HALF)
                sp.wait_ge(x2_stored[r], 16 * HALF + X2_STORED0)
            sp.wait_ge(y_added, Y_ADDED0)

            def load_tile(j, s):
                at = sp.value_load(tile_row[0:1, bass.ds(j, 1)], min_val=0,
                                   max_val=NE * REGION + (SPARE - 1) * P)
                sp.dma_start(xt[:, s], sorted_rows[bass.ds(at, P), :]).then_inc(tile_loaded[s], 16)

            for s in range(XR):
                load_tile(s, s)
            with sp.Fori(1, TILES // XR) as i:
                for s in range(XR):
                    sp.wait_ge(y_added, 16 * (XR * i + s - XR + 1) + Y_ADDED0)
                    load_tile(XR * i + s, s)
            for j in range(TILES // XR * XR, TILES):
                sp.wait_ge(y_added, 16 * (j - XR + 1) + Y_ADDED0)
                load_tile(j, j % XR)
            sp.wait_ge(y_added, 16 * TILES + Y_ADDED0)

        @block.gpsimd
        def _(pool):
            nc.gpsimd.memset(ident[:], 1.0)
            nc.gpsimd.memset(tri[:], 1.0)
            nc.gpsimd.memset(ones[:], 1.0)
            nc.gpsimd.memset(pad_tile[:], 0.0)
            nc.gpsimd.memset(one8[:], 1.0).then_inc(pool_consts, 1)
            pool.wait_ge(pool_consts, 1)
            nc.gpsimd.affine_select(out=ident[:], in_=ident[:], pattern=[[-1, P]], compare_op=ALU.is_equal,
                                    fill=0.0, base=0, channel_multiplier=1)
            nc.gpsimd.affine_select(out=tri[:], in_=tri[:], pattern=[[1, P]], compare_op=ALU.is_gt,
                                    fill=0.0, base=0, channel_multiplier=-1)
            for ramp, step, count, by_partition in ((kpos, 1, CTX, 0), (qpos, P, QT, 1), (iota_e, 1, NE, 0),
                                                    (region, REGION, NE, 0), (J, 1, TILES, 0), (tok, P, NT, 1),
                                                    (need, CUTS, NE, 0)):
                nc.gpsimd.iota(ramp[:], [[step, count]], base=2 if ramp is need else 0,
                               channel_multiplier=by_partition,
                               allow_small_or_imprecise_dtypes=True).then_inc(pool_consts, 1)
            nc.gpsimd.iota(pad_tile[:, TOK:TOK + 1].bitcast(I32), [[1, 1]], base=N,
                           channel_multiplier=1).then_inc(pads_ready, 1)
            pool.wait_ge(pads_ready, 1)
            spare = sorted_rows[NE * REGION:, :].rearrange("(k p) c -> p k c", p=P)
            for r, tiles in enumerate(((0, SPARE // 2), (SPARE // 2, SPARE))):
                count = tiles[1] - tiles[0]
                nc.gpsimd.dma_start(spare[:, tiles[0]:tiles[1], :],
                                    pad_tile[:].unsqueeze(1).to_broadcast([P, count, ROW])
                                    ).then_inc(scattered[r], SCATTERED0)
            nc.gpsimd.dma_start(out[N:N + P, :], pad_tile[:, 0:D]).then_inc(y_added, Y_ADDED0)

            def turn(k, r, i, behind):
                pool.wait_ge(rows_normed, k + 1 + NORMED0)
                pool.wait_ge(slots_ready, k + 1)
                pool.sem_inc(passed_pool)
                for t in range(G):
                    for e in range(TOPK):
                        nc.gpsimd.indirect_dma_start(
                            out=sorted_rows,
                            out_offset=bass.IndirectOffsetOnAxis(ap=slot[:, r, e, t:t + 1], axis=0),
                            in_=pay[:, r, t, :], in_offset=None).then_inc(scattered[r], 16)

            turns(pool, turn)

            def add(j, s):
                pool.wait_ge(y_ready, j + 1 + Y_READY0)
                pool.wait_ge(y_added, 16 * j + Y_ADDED0)
                pool.sem_inc(passed_pool)
                nc.gpsimd.indirect_dma_start(
                    out=out, out_offset=bass.IndirectOffsetOnAxis(ap=xt[:, s, TOK:TOK + 1].bitcast(I32), axis=0),
                    in_=y[:, s % 2, :], in_offset=None, compute_op=ALU.add).then_inc(y_added, 16)

            with pool.Fori(0, TILES // XR) as i:
                for s in range(XR):
                    add(XR * i + s, s)
            for j in range(TILES // XR * XR, TILES):
                add(j, j % XR)

        @block.scalar
        def _(act):
            act.sem_inc(y_ready, Y_READY0)
            act.wait_ge(small_loaded, SMALL)
            nc.scalar.activation(gates[:], graw[:], ACT.Tanh).then_inc(gates_ready, 1)
            nc.scalar.preload_act_table_set("natural_log_exp_and_others")
            for b in range(BATCH):
                act.wait_ge(krT_ready, b + 1)
                nc.scalar.copy(krT[:, b], O[:, b, 0:DC * KR].rearrange("p (c k) -> p c k", c=DC)).then_inc(krT_copied, 1)
            act.wait_ge(wr_ready, 1)
            nc.scalar.copy(brow[0:1, D:OW], R[0:1, 0:NE])
            nc.scalar.copy(wT_sb[:, :, D:OW], ET[:, 0:DC * NE].rearrange("p (c k) -> p c k", c=DC)).then_inc(wr_copied, 1)
            for b in range(BATCH):
                act.wait_ge(vw_ready, b + 1)
                nc.scalar.copy(vw[:, b], O[0:CTX, b, 0:OW]).then_inc(vw_copied, 1)

            def inverse_sqrt(k, r):
                act.wait_ge(var_ready, k + 3)
                nc.scalar.activation(lnv[:], ve[:, r], ACT.Ln).then_inc(ln_ready, 1)
                act.wait_ge(ln_ready, k + 3)
                nc.scalar.activation(rt0[:], lnv[:], ACT.Exp, scale=-0.5).then_inc(rsqrt_ready, 1)

            def exponentials(g, r):
                act.wait_ge(negmax_ready, g + 1)
                for t in range(G):
                    last = nc.scalar.activation(ex[:, r, t], sm[:, r, t], ACT.Exp, bias=nb[:, r, t:t + 1],
                                                scale=rt[:, r, t:t + 1], accum_out=rs[:, r, t:t + 1])
                last.then_inc(exp_ready, 1)

            def copy_expT(g):
                act.wait_ge(expT_ready, g + 1)
                nc.scalar.copy(eT[:], ET[0:CTX, :]).then_inc(expT_copied, 1)

            for g in range(2):
                inverse_sqrt(g - 2, g)
                exponentials(g, g)
                copy_expT(g)

            def turn(k, r, i, behind):
                def norm(t):
                    rows = xg[:, bass.ds(slot_of(r, i) + t, 1), :].rearrange("p t d -> p (t d)")
                    return nc.scalar.activation(pay[:, r, t, 0:D], rows, ACT.Identity,
                                                bias=nmr2[:, r, t:t + 1], scale=rstd2[:, r, t:t + 1])

                inverse_sqrt(k, r)
                if behind > 1:
                    exponentials(k + 2, r)
                act.wait_ge(gap_ready, k + 1)
                nc.scalar.activation(ed[:], dl[:], ACT.Exp).then_inc(gap_exp_ready, 1)
                act.wait_ge(bias2_ready, k + 1)
                act.wait_ge(scattered[r], 16 * TOPK * G * i + SCATTERED0)
                norm(0)
                norm(1)
                if behind > 1:
                    copy_expT(k + 2)
                norm(2)
                norm(3)
                nc.scalar.copy(pay[:, r, :, TOK].bitcast(I32), tok[:, bass.ds(k * G, G)]).then_inc(rows_normed, 1)

            turns(act, turn)

            def cut_high(e, h, at, size):
                return nc.scalar.copy(w_high[h][:, bass.ds(e * HW + at, size)],
                                      raw[h][:, bass.ds(e, 1), at:at + size].rearrange("p e n -> p (e n)"))

            def cut_all_high(e):
                for h in range(HALVES):
                    last = cut_high(e, h, 0, HW)
                last.then_inc(weight_high, 1)

            act.wait_ge(raw_loaded, 16 * HALVES * EARLY)
            cut_all_high(0)

            def tile_highs(j, s):
                act.wait_ge(tileT_ready, j + 1)
                nc.scalar.copy(xtT[:, s % 2, 0], XT[:, s % 2, 0:D]).then_inc(tile_high, 1)

            def silu(j, s):
                act.wait_ge(gate_ready, j + 1)
                nc.scalar.activation(hid[:], GT[:], ACT.Silu).then_inc(silu_ready, 1)

            def hidden_highs(j):
                act.wait_ge(hiddenT_ready, j + 1)
                nc.scalar.copy(hT[:, 0], HT[:]).then_inc(hidden_high, 1)

            def weigh(j, s, e):
                act.wait_ge(down_ready, j + 1)
                act.wait_ge(y_added, 16 * (j - 1) + Y_ADDED0)
                nc.scalar.mul(y[:, s % 2], Y[:, s % 2, 0:D], xt[:, s, bass.ds(e + CW, 1)]).then_inc(y_ready, 1)

            act.wait_ge(tables_ready, 1)
            is_skewed = act.value_load(skewed[:], min_val=0, max_val=1)
            with act.If(is_skewed == 1):
                act.wait_ge(raw_late, 16 * HALVES * (NE - EARLY))
                for r in range(2):
                    act.wait_ge(scattered[r], SCATTERED0 + 16 * TOPK * G * HALF)
                    act.wait_ge(x2_stored[r], 16 * HALF + X2_STORED0)
                for e in range(1, NE):
                    cut_all_high(e)
            tile_highs(0, 0)
            tile_highs(1, 1)
            silu(0, 0)

            def turn(j, s, after=2, piece_of=None):
                hidden_highs(j)
                e = act.value_load(tile_expert[0:1, bass.ds(j, 1)], min_val=0, max_val=NE - 1)
                if after > 0:
                    silu(j + 1, s + 1)
                if after > 1:
                    tile_highs(j + 2, s + 2)
                if piece_of is not None:
                    with act.If(is_skewed == 0):
                        at = s % CUTS * PIECE
                        cut_high(piece_of, at // HW, at % HW, PIECE).then_inc(weight_high, 1)
                weigh(j, s, e)

            act.wait_ge(raw_late, 16 * HALVES * (NE - EARLY))
            with act.Fori(0, NE // 2 - 1) as i:
                for s in range(XR):
                    turn(XR * i + s, s, piece_of=2 * i + 1 + s // CUTS)
            for s in range(XR):
                turn(XR * (NE // 2 - 1) + s, s, piece_of=NE - 1 if s < CUTS else None)
            with act.Fori(NE // 2, TURNS) as i:
                for s in range(XR):
                    turn(XR * i + s, s)
            for j in range(TURNS * XR, TILES):
                turn(j, j % XR, TILES - 1 - j)

        @block.vector
        def _(dve):
            tt, ts, stt = nc.vector.tensor_tensor, nc.vector.tensor_scalar, nc.vector.scalar_tensor_tensor

            def per_expert(v):
                return v.unsqueeze(2).to_broadcast([P, G, NE])

            def per_tile(v):
                return v.unsqueeze(1).to_broadcast([P, G, NE])

            nc.vector.memset(kr[:], 0.0).then_inc(kr_zeroed, 1)
            nc.vector.memset(carry[:], 0.0)
            nc.vector.memset(ve[:], 1.0)
            nc.vector.memset(ones_row[:], 1.0).then_inc(setup_steps, 1)
            dve.wait_ge(setup_steps, 1)
            dve.wait_ge(small_loaded, SMALL)
            for b in range(BATCH):
                last = nc.vector.bn_stats(kst[:, b], kr[:, b])
            last.then_inc(setup_steps, 1)
            dve.wait_ge(setup_steps, 2)
            for b in range(BATCH):
                last = nc.vector.bn_aggr(kmv[:, b], kst[:, b])
            last.then_inc(setup_steps, 1)
            dve.wait_ge(setup_steps, 3)
            for b in range(BATCH):
                ts(kr[:, b], kr[:, b], kmv[:, b, 0:1], None, ALU.subtract).then_inc(keys_centred, 1)
            nc.vector.tensor_copy(lens_f[:], lens_i[:]).then_inc(setup_steps, 1)
            dve.wait_ge(setup_steps, 4)
            dve.wait_ge(pool_consts, 8)
            for b in range(BATCH):
                ts(kmask[:, b * CTX:(b + 1) * CTX], kpos[:], lens_f[:, b:b + 1], MASKED, ALU.is_ge, ALU.mult)
                last = ts(qmask[:, b * QT:(b + 1) * QT], qpos[:], lens_f[:, b:b + 1], None, ALU.is_ge)
            last.then_inc(setup_steps, 1)
            dve.wait_ge(setup_steps, 5)
            dve.wait_ge(gates_ready, 1)

            base = [0, 0]

            def mark(ins):
                base[1] += 1
                ins.then_inc(dve_steps, 1)
                return base[1]

            def after(step):
                dve.wait_ge(dve_steps, base[0] + step)

            def rows(r, i, t):
                return xg[:, bass.ds(slot_of(r, i) + t, 1), :].rearrange("p t d -> p (t d)")

            def statistics(st, r, i):
                for t in range(G):
                    last = nc.vector.bn_stats(st[:, t], rows(r, i, t))
                return last

            def aggregates(mv, st):
                dve.sem_inc(passed_dve)
                for t in range(G):
                    last = nc.vector.bn_aggr(mv[:, t], st[:, t])
                return last

            def variances(out_, mv):
                return ts(out_, mv[:, :, 1], EPS, float(D), ALU.add, ALU.mult)

            def masked_scores(g, q, b):
                dve.wait_ge(scores_ready, g + 1)
                for t in range(G):
                    last = stt(out=sm[:, q, t], in0=kmask[:, bass.ds(b * CTX, CTX)],
                               scalar=qmask[:, bass.ds(g * G + t, 1)],
                               in1=S[:, q, t * KR:t * KR + CTX], op0=ALU.mult, op1=ALU.add)
                return last

            def router_part(q):
                nc.vector.tensor_copy(
                    sr[:, q], S[:, q, 0:G * KR].rearrange("p (t k) -> p t k", t=G)[:, :, CTX:CTX + NE]
                ).then_inc(scores_free, 1)

            def refine(k, r):
                dve.wait_ge(rsqrt_ready, k + 3)
                after(mark(tt(out=rt0sq[:], in0=rt0[:], in1=rt0[:], op=ALU.mult)))
                after(mark(tt(out=rt0v[:], in0=rt0sq[:], in1=ve[:, r], op=ALU.mult)))
                after(mark(ts(rt0c[:], rt0v[:], -0.5, 1.5, ALU.mult, ALU.add)))
                return mark(tt(out=rt[:, r], in0=rt0c[:], in1=rt0[:], op=ALU.mult))

            def negated_maxima(q):
                stt(out=nb[:, q], in0=mx[:], scalar=-1.0, in1=rt[:, q, 0:G],
                    op0=ALU.mult, op1=ALU.mult).then_inc(negmax_ready, 1)

            for g in range(2):
                dve.wait_ge(x_loaded[g], 16)
                after(mark(statistics(st1, g, 0)))
                after(mark(aggregates(mv1, st1)))
                variances(ve[:, g, 0:G], mv1).then_inc(var_ready, 1)
                scores0 = mark(masked_scores(g, g, 0))
                router_part(g)
                after(scores0)
                nc.vector.tensor_reduce(mx[:], sm[:, g], axis=AX.X, op=ALU.max)
                after(refine(g - 2, g))
                negated_maxima(g)
            first = base[1]

            def turn(k, r, i, behind):
                base[0] = base[0] + base[1] if behind == 0 else k * STEPS + first
                base[1] = 0
                dve.wait_ge(exp_ready, k + 1)
                inv = mark(nc.vector.reciprocal(rg[:], rs[:, r]))
                if behind > 1:
                    dve.wait_ge(x_loaded[r], 16 * (i + 1) + 16)
                    dve.sem_inc(passed_dve)
                    stats1 = mark(statistics(st1, r, i + 1))
                after(inv)
                factor = mark(ts(rgt[:], rg[:], gates[:, 0:1], None, ALU.mult))
                if behind > 1:
                    after(stats1)
                    moments1 = mark(aggregates(mv1, st1))
                after(factor)
                dve.wait_ge(attn_ready, k + 1)
                tt(out=lg0[:], in0=O[:, :, D:OW], in1=per_expert(rgt[:]), op=ALU.mult)
                for t in range(G):
                    last = stt(out=rows(r, i, t), in0=O[:, t, 0:D], scalar=rgt[:, t:t + 1], in1=rows(r, i, t),
                               op0=ALU.mult, op1=ALU.add)
                last.then_inc(attn_used, 1)
                if behind > 1:
                    after(moments1)
                    variances(ve[:, r, 0:G], mv1)
                dve.wait_ge(attn_used, k + 1)
                dve.sem_inc(passed_dve)
                stats2 = mark(statistics(st2, r, i))
                sums = mark(tt(out=lg1[:], in0=lg0[:], in1=sr[:, r], op=ALU.add))
                after(stats2)
                moments2 = mark(aggregates(mv2, st2))
                after(moments2)
                variances(ve[:, r, G:2 * G], mv2).then_inc(var_ready, 1)
                if behind > 1:
                    scores = mark(masked_scores(k + 2, r, i + 1))
                    router_part(r)
                    after(scores)
                    nc.vector.tensor_reduce(mx[:], sm[:, r], axis=AX.X, op=ALU.max)
                after(refine(k, r))
                if behind > 1:
                    negated_maxima(r)
                root = mark(ts(rstd2[:, r], rt[:, r, G:2 * G], float(D) ** 0.5, None, ALU.mult))
                after(root)
                logits = mark(tt(out=lg[:], in0=lg1[:], in1=per_expert(rstd2[:, r]), op=ALU.mult))
                stt(out=nmr2[:, r], in0=mv2[:, :, 0], scalar=-1.0, in1=rstd2[:, r],
                    op0=ALU.mult, op1=ALU.mult).then_inc(bias2_ready, 1)
                after(logits)
                dve.sem_inc(passed_dve)
                for t in range(G):
                    last = nc.vector.max(m8[:, t], lg[:, t])
                largest = mark(last)
                after(largest)
                tt(out=dl[:], in0=m8[:, :, 1], in1=m8[:, :, 0], op=ALU.subtract).then_inc(gap_ready, 1)
                for t in range(G):
                    last = nc.vector.max_index(mi[:, t], m8[:, t], lg[:, t])
                after(mark(last))
                for e in range(TOPK):
                    last = tt(out=oh[:, e], in0=per_tile(iota_e[:]), in1=per_expert(mi[:, :, e]), op=ALU.is_equal)
                after(mark(last))
                tt(out=picks[:], in0=oh[:, 0], in1=oh[:, 1], op=ALU.add).then_inc(picks_ready, 1)
                dve.wait_ge(gap_exp_ready, k + 1)
                above = mark(ts(ed1[:], ed[:], 1.0, None, ALU.add))
                dve.wait_ge(ranks_ready, k + 1)
                places = mark(tt(out=place[:], in0=R[:, 0:G * NE].rearrange("p (t e) -> p t e", t=G),
                                 in1=per_tile(region[:]), op=ALU.add))
                after(above)
                share = mark(nc.vector.reciprocal(rw[:], ed1[:]))
                after(places)
                for e in range(TOPK):
                    last = tt(out=po[:, e], in0=oh[:, e], in1=place[:], op=ALU.mult)
                own = mark(last)
                after(share)
                first_w = mark(ts(wk[:, 0], rw[:], gates[:, 1:2], None, ALU.mult))
                after(own)
                dve.wait_ge(scattered[r], 16 * TOPK * G * i + SCATTERED0)
                with nc.allow_low_precision(reason="whole numbers below 2**24, summed in float32"):
                    nc.vector.tensor_reduce(slot[:, r], po[:], axis=AX.X, op=ALU.add)
                after(first_w)
                second_w = mark(tt(out=wk[:, 1], in0=wk[:, 0], in1=ed[:], op=ALU.mult))
                dve.wait_ge(picks_ready, k + 1)
                counted = mark(nc.vector.tensor_reduce(npicks[:], picks[:].rearrange("p t e -> p e t"),
                                                       axis=AX.X, op=ALU.add))
                after(second_w)
                for e in range(TOPK):
                    last = tt(out=cw[:, e], in0=oh[:, e], in1=per_expert(wk[:, e]), op=ALU.mult)
                weighed = mark(last)
                after(counted)
                carried = mark(tt(out=carry[:], in0=carry[:], in1=npicks[:], op=ALU.add))
                after(weighed)
                tt(out=pay[:, r, :, CW:ROW], in0=cw[:, 0], in1=cw[:, 1], op=ALU.add).then_inc(slots_ready, 1)
                assert behind < 2 or base[1] == STEPS, base[1]

            turns(dve, turn)

            done = [0]

            def step(ins):
                done[0] += 1
                ins.then_inc(table_steps, 1)
                dve.wait_ge(table_steps, done[0])

            dve.wait_ge(counts_ready, 1)
            nc.vector.tensor_copy(cnt[:], R[0:1, 0:NE])
            step(ts(nti[:], R[0:1, 0:NE], float(P - 1), None, ALU.add))
            tt(out=pad_row[:], in0=region[0:1, :], in1=cnt[:], op=ALU.add)
            step(nc.vector.tensor_single_scalar(nts[:], nti[:], P.bit_length() - 1, ALU.logical_shift_right))
            step(nc.vector.tensor_copy(ntf[:], nts[:]))
            step(nc.vector.tensor_tensor_scan(cum[:], one8[:], ntf[:], 0.0, ALU.mult, ALU.add))
            tt(out=start[:], in0=cum[:], in1=ntf[:], op=ALU.subtract)
            step(tt(out=past[:], in0=J[:].unsqueeze(2).to_broadcast([1, TILES, NE]),
                    in1=cum[:].unsqueeze(1).to_broadcast([1, TILES, NE]), op=ALU.is_ge))
            tt(out=soon[:], in0=start[:], in1=need[:], op=ALU.is_lt)
            nc.vector.tensor_reduce(tex[:], past[:], axis=AX.X, op=ALU.add)
            step(tt(out=pastn[:], in0=past[:], in1=ntf[:].unsqueeze(1).to_broadcast([1, TILES, NE]), op=ALU.mult))
            nc.vector.tensor_reduce(skew_f[:], soon[0:1, 1:NE], axis=AX.X, op=ALU.max)
            step(nc.vector.tensor_reduce(before[:], pastn[:], axis=AX.X, op=ALU.add))
            nc.vector.tensor_copy(skewed[:], skew_f[:])
            step(tt(out=rel[:], in0=J[:], in1=before[:], op=ALU.subtract))
            step(ts(rel128[:], rel[:], float(P), None, ALU.mult))
            ts(tile_expert[:], tex[:], float(NE - 1), None, ALU.min)
            stt(out=tile_row[:], in0=tex[:], scalar=float(REGION), in1=rel128[:],
                op0=ALU.mult, op1=ALU.add).then_inc(tables_ready, 1)

            def cut_low(e, h, at, size):
                return tt(out=w_low[h][:, bass.ds(e * HW + at, size)],
                          in0=raw[h][:, bass.ds(e, 1), at:at + size].rearrange("p e n -> p (e n)"),
                          in1=w_high[h][:, bass.ds(e * HW + at, size)].bitcast(F32), op=ALU.subtract)

            def cut_all_low(e):
                dve.wait_ge(weight_high, e + 1)
                for h in range(HALVES):
                    last = cut_low(e, h, 0, HW)
                last.then_inc(weight_low, 1)

            cut_all_low(0)

            def tile_lows(j, s):
                dve.wait_ge(tile_high, j + 1)
                tt(out=xtT[:, s % 2, 1], in0=XT[:, s % 2, 0:D], in1=xtT[:, s % 2, 0].bitcast(F32),
                   op=ALU.subtract).then_inc(tile_low, 1)

            def gate_up(j, s):
                dve.wait_ge(up_ready, j + 1)
                tt(out=hid[:], in0=hid[:], in1=UP[:], op=ALU.mult).then_inc(hidden_ready, 1)

            def hidden_lows(j):
                dve.wait_ge(hidden_high, j + 1)
                tt(out=hT[:, 1], in0=HT[:], in1=hT[:, 0].bitcast(F32), op=ALU.subtract).then_inc(hidden_low, 1)

            is_skewed = dve.value_load(skewed[:], min_val=0, max_val=1)
            with dve.If(is_skewed == 1):
                for e in range(1, NE):
                    cut_all_low(e)
            tile_lows(0, 0)
            tile_lows(1, 1)
            dve.wait_ge(silu_ready, 1)
            gate_up(0, 0)

            def turn(j, s, after=2, piece_of=None):
                hidden_lows(j)
                if after > 1:
                    tile_lows(j + 2, s + 2)
                if after == 1:
                    dve.wait_ge(silu_ready, j + 2)
                if after > 0:
                    gate_up(j + 1, s + 1)
                if piece_of is not None:
                    with dve.If(is_skewed == 0):
                        dve.wait_ge(weight_high, j + 2)
                        at = s % CUTS * PIECE
                        last = cut_low(piece_of, at // HW, at % HW, PIECE)
                        if s % CUTS == CUTS - 1:
                            last.then_inc(weight_low, 1)

            with dve.Fori(0, NE // 2 - 1) as i:
                for s in range(XR):
                    turn(XR * i + s, s, piece_of=2 * i + 1 + s // CUTS)
            for s in range(XR):
                turn(XR * (NE // 2 - 1) + s, s, piece_of=NE - 1 if s < CUTS else None)
            with dve.Fori(NE // 2, TURNS) as i:
                for s in range(XR):
                    turn(XR * i + s, s)
            for j in range(TURNS * XR, TILES):
                turn(j, j % XR, TILES - 1 - j)

        @block.tensor
        def _(pe):
            mm = nc.tensor.matmul
            pe.wait_ge(pool_consts, 2)
            for b in range(BATCH):
                pe.wait_ge(keys_centred, b + 1)
                for c in range(DC):
                    last = nc.tensor.transpose(O[:, b, c * KR:(c + 1) * KR], kr[:, b, c * P:(c + 1) * P],
                                               ident[0:KR, 0:KR])
                last.then_inc(krT_ready, 1)
            pe.wait_ge(krT_copied, BATCH)

            def scores(g, r, b):
                for t in range(G):
                    for c in range(DC):
                        last = mm(S[:, r, t * KR:(t + 1) * KR], xTg[:, r, c, t * P:(t + 1) * P],
                                  krT[:, bass.ds(b, 1), c, :].rearrange("p b k -> p (b k)"),
                                  start=(c == 0), stop=(c == DC - 1))
                last.then_inc(scores_ready, 1)

            pe.wait_ge(small_loaded, SMALL)
            routerT = krT[:, 0, :, CTX:CTX + NE]
            for dc in range(DC):
                for c in range(DC):
                    mm(ET[:, dc * NE:(dc + 1) * NE], w_sb[:, c, dc * P:(dc + 1) * P], routerT[:, c],
                       start=(c == 0), stop=(c == DC - 1))
            for c in range(DC):
                last = mm(R[0:1, 0:NE], bcol[:, c:c + 1], routerT[:, c], start=(c == 0), stop=(c == DC - 1))
            last.then_inc(wr_ready, 1)
            for g in range(2):
                pe.wait_ge(xT_loaded[g], 16)
                scores(g, g, 0)
            pe.wait_ge(wr_copied, 1)
            for b in range(BATCH):
                for c in range(DC):
                    mm(O[0:CTX, b, 0:OW], ctxT_sb[:, c, b * CTX:(b + 1) * CTX], wT_sb[:, c], start=(c == 0), stop=False)
                mm(O[0:CTX, b, 0:OW], ones_row[:], brow[:], start=False, stop=True).then_inc(vw_ready, 1)
            pe.wait_ge(vw_copied, BATCH)

            def transpose_exp(g, r):
                pe.wait_ge(exp_ready, g + 1)
                for t in range(G):
                    last = nc.tensor.transpose(ET[0:CTX, t * P:(t + 1) * P], ex[:, r, t], ident[:])
                last.then_inc(expT_ready, 1)

            def attention(g, b):
                pe.wait_ge(expT_copied, g + 1)
                for t in range(G):
                    last = mm(O[:, t, 0:OW], eT[:, t * P:(t + 1) * P],
                              vw[:, bass.ds(b, 1), :].rearrange("p b k -> p (b k)"), start=True, stop=True)
                last.then_inc(attn_ready, 1)

            transpose_exp(0, 0)
            attention(0, 0)
            transpose_exp(1, 1)

            def turn(k, r, i, behind):
                if behind > 1:
                    pe.wait_ge(xT_loaded[r], 16 * i + 32)
                    pe.wait_ge(scores_free, k + 1)
                    scores(k + 2, r, i + 1)
                if behind > 0:
                    pe.wait_ge(attn_used, k + 1)
                    attention(k + 1, i + r)
                pe.wait_ge(picks_ready, k + 1)
                ranks = R[:, 0:G * NE].rearrange("p (t e) -> p t e", t=G)
                mm(ranks, ones[:], carry[:].unsqueeze(1).to_broadcast([P, G, NE]), start=True, stop=False)
                for t in range(G - 1):
                    mm(ranks[:, t + 1:G], ones[:], picks[:, t:t + 1].to_broadcast([P, G - 1 - t, NE]),
                       start=False, stop=False, skip_group_check=True)
                mm(ranks, tri[:], picks[:], start=False, stop=True).then_inc(ranks_ready, 1)
                if behind > 1:
                    transpose_exp(k + 2, r)

            turns(pe, turn)

            pe.wait_ge(slots_ready, GROUPS)
            mm(R[:, 0:NE], ones[:], carry[:], start=True, stop=True).then_inc(counts_ready, 1)

            def expert(j):
                return pe.value_load(tile_expert[0:1, bass.ds(j, 1)], min_val=0, max_val=NE - 1)

            def transpose_tile(s):
                for c in range(DC):
                    last = nc.tensor.transpose(XT[:, s % 2, c * P:(c + 1) * P], xt[:, s % XR, c * P:(c + 1) * P], ident[:])
                last.then_inc(tileT_ready, 1)

            parts = (w_high, w_low)
            HI_LO = ((0, 0), (0, 1), (1, 0))

            def first_layer(bank, s, e, k):
                for c in range(DC):
                    for n, (px, pw) in enumerate(HI_LO):
                        last = mm(bank[:], xtT[:, s % 2, px, c * P:(c + 1) * P],
                                  parts[pw][c][:, bass.ds(e * HW + k * HID, HID)],
                                  start=(c == 0 and n == 0), stop=(c == DC - 1 and n == 2))
                return last

            def gate(j, s, e):
                pe.wait_ge(tile_low, j + 1)
                first_layer(GT, s, e, 0).then_inc(gate_ready, 1)

            def up(j, s, e):
                first_layer(UP, s, e, 1).then_inc(up_ready, 1)

            def transpose_hidden(j, s):
                pe.wait_ge(hidden_ready, j + 1)
                for c in range(HC):
                    last = nc.tensor.transpose(HT[:, c * P:(c + 1) * P], hid[:, c * P:(c + 1) * P], ident[:])
                last.then_inc(hiddenT_ready, 1)

            def down(j, s, e):
                pe.wait_ge(hidden_low, j + 1)
                for px in range(2):
                    for c in range(HC):
                        for pw in range(2 - px):
                            last = mm(Y[:, s % 2, 0:D], hT[:, px, c * P:(c + 1) * P],
                                      parts[pw][c // (HC // DC)][:, bass.ds(e * HW + DOWN + c % (HC // DC) * D, D)],
                                      start=(px == 0 and c == 0 and pw == 0), stop=(px == 1 and c == HC - 1))
                last.then_inc(down_ready, 1)

            def turn(j, s, turns, e=None, e1=None, after=2):
                e2 = None
                transpose_hidden(j, s)
                if after > 0:
                    if e1 is None:
                        e1 = expert(j + 1)
                    gate(j + 1, s + 1, e1)
                if after > 1:
                    pe.wait_ge(tile_loaded[(s + 2) % XR], 16 * (turns + 1 + (s + 2) // XR))
                    transpose_tile(s + 2)
                if after > 0:
                    up(j + 1, s + 1, e1)
                if after > 1:
                    e2 = expert(j + 2)
                if e is None:
                    e = expert(j)
                down(j, s, e)
                return e1, e2

            pe.wait_ge(tables_ready, 1)
            e = expert(0)
            for j in range(2):
                pe.wait_ge(tile_loaded[j], 16)
                transpose_tile(j)
            gate(0, 0, e)
            up(0, 0, e)
            with pe.Fori(0, TURNS) as i:
                e, e1 = None, None
                for s in range(XR):
                    e, e1 = turn(XR * i + s, s, i, e, e1)
            e, e1 = None, None
            for j in range(TURNS * XR, TILES):
                e, e1 = turn(j, j % XR, TURNS, e, e1, TILES - 1 - j)


def kernel(x, ctx_1024, _lenS2, g_xattn, g_ffn, L0_xattn_W, L0_xattn_b, L0_ffn_router_w, L0_ffn_w_gate,
           L0_ffn_w_up, L0_ffn_w_down):
    import numpy as np
    import concourse.bacc as bacc
    from concourse.bass_utils import run_bass_kernel_spmd

    rows = np.asarray(x).reshape(N, D)
    ctx = np.asarray(ctx_1024)
    W = np.asarray(L0_xattn_W)
    b = np.asarray(L0_xattn_b)

    def by_chunk(w):
        e, rows_, cols = w.shape
        return w.reshape(e, rows_ // P, P, cols).transpose(0, 2, 1, 3)

    gate, up, down = (by_chunk(np.asarray(w).transpose(0, 2, 1)) for w in (L0_ffn_w_gate, L0_ffn_w_up, L0_ffn_w_down))
    weights = np.concatenate([np.stack([gate, up], axis=3).reshape(NE, P, HALVES, DOWN),
                              down.reshape(NE, P, HALVES, HW - DOWN)], axis=3)
    laid_out = {
        "x": rows, "xT": rows.T,
        "ctx_rows": ctx, "ctxT": ctx.reshape(BATCH * CTX, D).T,
        "lens": np.asarray(_lenS2).reshape(1, BATCH),
        "g_x": np.asarray(g_xattn).reshape(1, 1), "g_f": np.asarray(g_ffn).reshape(1, 1),
        "w_rows": W, "wT": W.T, "b_row": b.reshape(1, D), "b_col": b.reshape(DC, P).T,
        "router": np.asarray(L0_ffn_router_w), "weights": weights,
    }
    nc = bacc.Bacc("TRN2", target_bir_lowering=False, num_devices=1, dynamic_dma_scratch_size=4096)
    arrays, args = {}, []
    for name, a in laid_out.items():
        a = np.ascontiguousarray(a)
        arrays[f"in_{name}"] = a
        args.append(nc.dram_tensor(f"in_{name}", a.shape, mybir.dt.from_np(a.dtype), kind="ExternalInput").ap())
    args.append(nc.dram_tensor("out_rows", (N + P, D), F32, kind="ExternalOutput").ap())
    moe_flamingo(nc, *args)
    r = run_bass_kernel_spmd(nc, [arrays], core_ids=[0])
    return r.results[0]["out_rows"][:N].reshape(BATCH, SEQ, D)
```

```python
import concourse.bass as bass
from concourse import mybir
from contextlib import ExitStack

F32 = mybir.dt.float32
F32R = mybir.dt.float32r
BF16 = mybir.dt.bfloat16
I32 = mybir.dt.int32
U32 = mybir.dt.uint32
ALU = mybir.AluOpType
ACT = mybir.ActivationFunctionType
AX = mybir.AxisListType

P = 128
BATCH, SEQ, D = 4, 1024, 256
CTX = 77
NE, HID, TOPK = 8, 512, 2
N = BATCH * SEQ
DC, HC = D // P, HID // P
G = 4
GROUPS = N // (G * P)
HALF = GROUPS // 2
NT = N // P
QT = SEQ // P
KR = 96
OW = D + NE
EPS = 1e-5
MASKED = -float(2 ** 100)

REGION = N + P
TILES = (TOPK * N - NE) // P + NE
SPARE = TILES - TOPK * N // P
ROW = D + 1 + NE
TOK, CW = D, D + 1
XR = 8
TURNS = (TILES - 2) // XR
DOWN = 2 * HID
HALVES, HW = DC, DOWN + HC // DC * D
CUTS = 4
PIECE = HALVES * HW // CUTS
EARLY = 3


def moe_flamingo(nc, x, xT, ctx_rows, ctxT, lens, g_x, g_f, w_rows, wT, b_row, b_col, router, weights, out):
    sorted_rows = nc.dram_tensor("sorted_rows", (NE * REGION + SPARE * P, ROW), F32, kind="Internal").ap()
    es = ExitStack()
    with es:
        def sb(name, shape, dt=F32, stack=es):
            return stack.enter_context(nc.sbuf_tensor(name, shape, dt))

        def pb(name, shape, stack):
            return stack.enter_context(nc.psum_tensor(name, shape, F32))

        def sem(name):
            return es.enter_context(nc.semaphore(name))

        ident = sb("ident", [P, P])
        gates = sb("gates", [P, 2])
        tile_expert = sb("tile_expert", [1, TILES], I32)
        tile_row = sb("tile_row", [1, TILES], I32)
        pad_row = sb("pad_row", [1, NE], I32)
        skewed = sb("skewed", [1, 1], I32)
        tiles_used = sb("tiles_used", [1, 1], I32)
        pad_tile = sb("pad_tile", [P, ROW])

        lo = ExitStack()
        raw = [sb(f"raw{h}", [P, NE, HW], F32, lo) for h in range(HALVES)]
        lo.close()
        w_low = [sb(f"w_low{h}", [P, NE * HW], F32R) for h in range(HALVES)]
        w_high0 = sb("w_high0", [P, NE * HW], F32R)

        a = ExitStack()
        ctxT_sb = sb("ctxT_sb", [P, DC, BATCH * CTX], F32, a)
        w_sb = sb("w_sb", [P, DC, D], F32, a)
        wT_sb = sb("wT_sb", [P, DC, OW], F32, a)
        xg = sb("xg", [P, 4 * G, D], F32, a)
        xTg = sb("xTg", [P, 2, DC, G * P], F32, a)
        pay = sb("pay", [P, 2, G, ROW], F32, a)
        kr = sb("kr", [KR, BATCH, D], F32, a)
        krT = sb("krT", [P, BATCH, DC, KR], F32, a)
        brow = sb("brow", [1, OW], F32, a)
        bcol = sb("bcol", [P, DC], F32, a)
        ones_row = sb("ones_row", [1, CTX], F32, a)
        vw = sb("vw", [CTX, BATCH, OW], F32, a)
        kst = sb("kst", [KR, BATCH, 6], F32, a)
        kmv = sb("kmv", [KR, BATCH, 2], F32, a)
        lens_i = sb("lens_i", [P, BATCH], I32, a)
        lens_f = sb("lens_f", [P, BATCH], F32, a)
        graw = sb("graw", [P, 2], F32, a)
        kpos = sb("kpos", [P, CTX], F32, a)
        qpos = sb("qpos", [P, QT], F32, a)
        kmask = sb("kmask", [P, BATCH * CTX], F32, a)
        qmask = sb("qmask", [P, NT], F32, a)
        tri = sb("tri", [P, P], BF16, a)
        ones = sb("ones", [P, P], BF16, a)
        iota_e = sb("iota_e", [P, NE], F32, a)
        region = sb("region", [P, NE], F32, a)
        tok = sb("tok", [P, NT], I32, a)
        st1 = sb("st1", [P, G, 6], F32, a)
        mv = sb("mv", [P, 2, G, 2], F32, a)
        sm = sb("sm", [P, 2, G, CTX], F32, a)
        mx = sb("mx", [P, G], F32, a)
        ve = sb("ve", [P, 2, 2 * G], F32, a)
        lnv = sb("lnv", [P, 2 * G], F32, a)
        rt0 = sb("rt0", [P, 2 * G], F32, a)
        rt0v = sb("rt0v", [P, 2 * G], F32, a)
        rt0c = sb("rt0c", [P, 2 * G], F32, a)
        rt = sb("rt", [P, 2, 2 * G], F32, a)
        nb = sb("nb", [P, 2, G], F32, a)
        sr = sb("sr", [P, 2, G, NE], F32, a)
        ex = sb("ex", [P, 2, G, CTX], F32, a)
        rs = sb("rs", [P, 2, G], F32, a)
        eT = sb("eT", [CTX, G * P], F32, a)
        rg = sb("rg", [P, G], F32, a)
        rgt = sb("rgt", [P, G], F32, a)
        lg0 = sb("lg0", [P, G, NE], F32, a)
        lg1 = sb("lg1", [P, G, NE], F32, a)
        lg = sb("lg", [P, G, NE], F32, a)
        st2 = sb("st2", [P, G, 6], F32, a)
        rstd2 = sb("rstd2", [P, 2, G], F32, a)
        nmr2 = sb("nmr2", [P, 2, G], F32, a)
        m8 = sb("m8", [P, G, NE], F32, a)
        mi = sb("mi", [P, G, NE], U32, a)
        oh = sb("oh", [P, TOPK, G, NE], F32, a)
        picks = sb("picks", [P, G, NE], BF16, a)
        npicks = sb("npicks", [P, NE], F32, a)
        carry = sb("carry", [P, NE], BF16, a)
        dl = sb("dl", [P, G], F32, a)
        ed = sb("ed", [P, G], F32, a)
        ed1 = sb("ed1", [P, G], F32, a)
        rw = sb("rw", [P, G], F32, a)
        wk = sb("wk", [P, TOPK, G], F32, a)
        cw = sb("cw", [P, TOPK, G, NE], F32, a)
        place = sb("place", [P, G, NE], F32, a)
        po = sb("po", [P, TOPK, G, NE], F32, a)
        slot = sb("slot", [P, 2, TOPK, G], I32, a)
        need = sb("need", [1, NE], F32, a)
        start = sb("start", [1, NE], F32, a)
        skew_f = sb("skew_f", [1, 1], F32, a)
        soon = sb("soon", [1, NE], F32, a)
        J = sb("J", [1, TILES], F32, a)
        cnt = sb("cnt", [1, NE], F32, a)
        nti = sb("nti", [1, NE], I32, a)
        nts = sb("nts", [1, NE], I32, a)
        ntf = sb("ntf", [1, NE], F32, a)
        cum = sb("cum", [1, NE], F32, a)
        one8 = sb("one8", [1, NE], F32, a)
        past = sb("past", [1, TILES, NE], F32, a)
        pastn = sb("pastn", [1, TILES, NE], F32, a)
        tex = sb("tex", [1, TILES], F32, a)
        before = sb("before", [1, TILES], F32, a)
        rel = sb("rel", [1, TILES], F32, a)
        rel128 = sb("rel128", [1, TILES], F32, a)
        S = pb("S", [P, 2, 512], a)
        ET = pb("ET", [P, 512], a)
        R = pb("R", [P, 512], a)
        O = pb("O", [P, G, 512], a)
        a.close()

        w_high = [w_high0, sb("w_high1", [P, NE * HW], F32R)]
        xt = sb("xt", [P, XR, ROW])
        xtT = sb("xtT", [P, 2, 2, D], F32R)
        hid = sb("hid", [P, HID])
        hT = sb("hT", [P, 2, HID], F32R)
        y = sb("y", [P, 2, D])
        XT = pb("XT", [P, 2, 512], es)
        GT = pb("GT", [P, 512], es)
        UP = pb("UP", [P, 512], es)
        HT = pb("HT", [P, 512], es)
        Y = pb("Y", [P, 2, 512], es)

        kr_zeroed = sem("kr_zeroed")
        small_loaded = sem("small_loaded")
        pool_consts = sem("pool_consts")
        pads_ready = sem("pads_ready")
        setup_steps = sem("setup_steps")
        keys_centred = sem("keys_centred")
        krT_ready = sem("krT_ready")
        krT_copied = sem("krT_copied")
        wr_ready = sem("wr_ready")
        wr_copied = sem("wr_copied")
        vw_ready = sem("vw_ready")
        vw_copied = sem("vw_copied")
        gates_ready = sem("gates_ready")
        raw_loaded = sem("raw_loaded")
        raw_late = sem("raw_late")
        dve_steps = sem("dve_steps")
        var_ready = sem("var_ready")
        ln_ready = sem("ln_ready")
        rsqrt_ready = sem("rsqrt_ready")
        scores_ready = sem("scores_ready")
        scores_free = sem("scores_free")
        negmax_ready = sem("negmax_ready")
        exp_ready = sem("exp_ready")
        expT_ready = sem("expT_ready")
        expT_copied = sem("expT_copied")
        attn_ready = sem("attn_ready")
        attn_used = sem("attn_used")
        bias2_ready = sem("bias2_ready")
        rows_normed = sem("rows_normed")
        gap_ready = sem("gap_ready")
        gap_exp_ready = sem("gap_exp_ready")
        picks_ready = sem("picks_ready")
        ranks_ready = sem("ranks_ready")
        slots_ready = sem("slots_ready")
        counts_ready = sem("counts_ready")
        table_steps = sem("table_steps")
        tables_ready = sem("tables_ready")
        pad_rows_ready = sem("pad_rows_ready")
        keys_loaded = sem("keys_loaded")
        values_loaded = sem("values_loaded")
        pads_written = sem("pads_written")
        tileT_ready = sem("tileT_ready")
        tile_high = sem("tile_high")
        tile_low = sem("tile_low")
        gate_ready = sem("gate_ready")
        silu_ready = sem("silu_ready")
        up_ready = sem("up_ready")
        hidden_ready = sem("hidden_ready")
        hiddenT_ready = sem("hiddenT_ready")
        hidden_high = sem("hidden_high")
        hidden_low = sem("hidden_low")
        down_ready = sem("down_ready")
        y_ready = sem("y_ready")
        y_added = sem("y_added")
        weight_high = sem("weight_high")
        weight_low = sem("weight_low")
        passed_sp = sem("passed_sp")
        passed_pool = sem("passed_pool")
        passed_dve = sem("passed_dve")
        passed_act = sem("passed_act")
        x_loaded = [sem(f"x_loaded{i}") for i in range(2)]
        xT_loaded = [sem(f"xT_loaded{i}") for i in range(2)]
        x2_stored = [sem(f"x2_stored{i}") for i in range(2)]
        scattered = [sem(f"scattered{i}") for i in range(2)]
        tile_loaded = [sem(f"tile_loaded{i}") for i in range(XR)]

        SCATTERED0 = 16 * TOPK * G
        X2_STORED0 = 16
        RAW_LATE0 = 16 * HALVES * 2
        NORMED0 = 2
        Y_READY0 = 2
        Y_ADDED0 = 16 * 2
        KEYS, SMALL, VALUES = 16 * 2, 16 * 3, 16 * 5
        STEPS = 25

        def turns(eng, turn):
            with eng.Fori(0, HALF - 1) as i:
                turn(2 * i, 0, i, 2)
                turn(2 * i + 1, 1, i, 2)
            turn(GROUPS - 2, 0, HALF - 1, 1)
            turn(GROUPS - 1, 1, HALF - 1, 0)

        def slot_of(r, i):
            return (i % 2) * (2 * G) + r * G

        def last_tiles(eng, tile):
            used = eng.value_load(tiles_used[:], min_val=TOPK * N // P, max_val=TILES)

            def rest(j):
                if j < TILES:
                    with eng.If(used > j):
                        tile(j)
                        rest(j + 1)

            rest(TURNS * XR)
            return used

        block = es.enter_context(nc.Block())

        @block.sync
        def _(sp):
            x_v = x.rearrange("(n p) d -> p n d", p=P)
            out_v = out[0:N, :].rearrange("(n p) d -> p n d", p=P)
            xT_v = xT.rearrange("(c p) n -> p c n", p=P)

            def load_x(g, r, i):
                sp.dma_start(xg[:, bass.ds(slot_of(r, i), G)], x_v[:, bass.ds(g * G, G), :]).then_inc(x_loaded[r], 16)

            def load_xT(g, r):
                sp.dma_start(xTg[:, r], xT_v[:, :, bass.ds(g * (G * P), G * P)]).then_inc(xT_loaded[r], 16)

            def load_weights(e, done):
                for h in range(HALVES):
                    sp.dma_start(raw[h][:, bass.ds(e, 1), :].rearrange("p e n -> p (e n)"),
                                 weights[bass.ds(e, 1), :, h].rearrange("e p n -> p (e n)")).then_inc(done, 16)

            def small(dst, src):
                sp.dma_start(dst, src).then_inc(small_loaded, 16)

            sp.sem_inc(x2_stored[0], X2_STORED0)
            sp.sem_inc(x2_stored[1], X2_STORED0)
            sp.sem_inc(rows_normed, NORMED0)
            sp.wait_ge(kr_zeroed, 1)
            sp.dma_start(kr[0:CTX, :, :], ctx_rows.rearrange("b k d -> k b d")).then_inc(keys_loaded, 16)
            sp.dma_start(kr[CTX:CTX + NE, :, :], router.unsqueeze(1).to_broadcast([NE, BATCH, D])).then_inc(keys_loaded, 16)
            small(lens_i[:], lens.to_broadcast([P, BATCH]))
            small(graw[:, 0:1], g_x.to_broadcast([P, 1]))
            small(graw[:, 1:2], g_f.to_broadcast([P, 1]))
            for g in range(2):
                load_x(g, g, 0)
                load_xT(g, g)
            def turn(k, r, i, behind):
                if behind > 1:
                    sp.wait_ge(var_ready, k + 1)
                    sp.wait_ge(x2_stored[r], 16 * i + X2_STORED0)
                    sp.wait_ge(rows_normed, k - 1 + NORMED0)
                    load_x(k + 2, r, i + 1)
                    sp.wait_ge(scores_ready, k + 1)
                    sp.sem_inc(passed_sp)
                    load_xT(k + 2, r)
                    if r == 1:
                        load_weights(i, raw_loaded)
                sp.wait_ge(attn_used, k + 1)
                sp.sem_inc(passed_sp)
                sp.dma_start(out_v[:, bass.ds(k * G, G), :], xg[:, bass.ds(slot_of(r, i), G)]).then_inc(x2_stored[r], 16)

            turns(sp, turn)

            sp.wait_ge(pad_rows_ready, 1)
            for e in range(NE):
                at = sp.value_load(pad_row[0:1, e:e + 1], min_val=0, max_val=NE * REGION - P)
                sp.dma_start(sorted_rows[bass.ds(at, P), :], pad_tile[:]).then_inc(pads_written, 16)

            def first_row(j):
                return sp.value_load(tile_row[0:1, bass.ds(j, 1)], min_val=0,
                                     max_val=NE * REGION + (SPARE - 1) * P)

            def load_tile(at, s):
                sp.dma_start(xt[:, s], sorted_rows[bass.ds(at, P), :]).then_inc(tile_loaded[s], 16)

            sp.wait_ge(tables_ready, 1)
            is_skewed = sp.value_load(skewed[:], min_val=0, max_val=1)
            first_rows = [first_row(j) for j in range(XR)]
            sp.wait_ge(pads_written, 16 * NE)
            for r in range(2):
                sp.wait_ge(scattered[r], SCATTERED0 + 16 * TOPK * G * HALF)
                sp.wait_ge(x2_stored[r], 16 * HALF + X2_STORED0)
            sp.wait_ge(y_added, Y_ADDED0)
            for j in range(XR):
                load_tile(first_rows[j], j)
            sp.sem_inc(raw_late, RAW_LATE0)
            load_weights(EARLY, raw_late)
            load_weights(EARLY + 1, raw_late)
            with sp.If(is_skewed == 1):
                for e in range(EARLY + 2, NE):
                    load_weights(e, raw_late)
            with sp.Fori(1, TILES // XR) as i:
                turn_or_none = i + TILES * is_skewed
                with sp.If(turn_or_none == 2):
                    load_weights(EARLY + 2, raw_late)
                    load_weights(EARLY + 3, raw_late)
                with sp.If(turn_or_none == 3):
                    load_weights(EARLY + 4, raw_late)
                for s in range(XR):
                    sp.wait_ge(y_added, 16 * (XR * i + s - XR + 1) + Y_ADDED0)
                    load_tile(first_row(XR * i + s), s)
            for j in range(TILES // XR * XR, TILES):
                sp.wait_ge(y_added, 16 * (j - XR + 1) + Y_ADDED0)
                load_tile(first_row(j), j % XR)
            for s in range(XR):
                sp.wait_ge(tile_loaded[s], 16 * ((TILES - 1 - s) // XR + 1))
            used = sp.value_load(tiles_used[:], min_val=TOPK * N // P, max_val=TILES)
            sp.wait_ge(y_added, 16 * used + Y_ADDED0)
            sp.sem_inc(passed_sp)

        @block.gpsimd
        def _(pool):
            nc.gpsimd.memset(ident[:], 1.0)
            nc.gpsimd.memset(tri[:], 1.0)
            nc.gpsimd.memset(ones[:], 1.0)
            nc.gpsimd.memset(pad_tile[:], 0.0)
            nc.gpsimd.memset(one8[:], 1.0).then_inc(pool_consts, 1)
            pool.wait_ge(pool_consts, 1)
            nc.gpsimd.affine_select(out=ident[:], in_=ident[:], pattern=[[-1, P]], compare_op=ALU.is_equal,
                                    fill=0.0, base=0, channel_multiplier=1)
            nc.gpsimd.affine_select(out=tri[:], in_=tri[:], pattern=[[1, P]], compare_op=ALU.is_gt,
                                    fill=0.0, base=0, channel_multiplier=-1)
            for ramp, step, count, by_partition in ((kpos, 1, CTX, 0), (qpos, P, QT, 1), (iota_e, 1, NE, 0),
                                                    (region, REGION, NE, 0), (J, 1, TILES, 0), (tok, P, NT, 1),
                                                    (need, CUTS, NE, 0)):
                nc.gpsimd.iota(ramp[:], [[step, count]], base=2 if ramp is need else 0,
                               channel_multiplier=by_partition,
                               allow_small_or_imprecise_dtypes=True).then_inc(pool_consts, 1)
            nc.gpsimd.iota(pad_tile[:, TOK:TOK + 1].bitcast(I32), [[1, 1]], base=N,
                           channel_multiplier=1).then_inc(pads_ready, 1)
            pool.wait_ge(pads_ready, 1)
            spare = sorted_rows[NE * REGION:, :].rearrange("(k p) c -> p k c", p=P)
            for r, tiles in enumerate(((0, SPARE // 2), (SPARE // 2, SPARE))):
                count = tiles[1] - tiles[0]
                nc.gpsimd.dma_start(spare[:, tiles[0]:tiles[1], :],
                                    pad_tile[:].unsqueeze(1).to_broadcast([P, count, ROW])
                                    ).then_inc(scattered[r], SCATTERED0)
            nc.gpsimd.dma_start(out[N:N + P, :], pad_tile[:, 0:D]).then_inc(y_added, Y_ADDED0)

            def turn(k, r, i, behind):
                pool.wait_ge(rows_normed, k + 1 + NORMED0)
                pool.wait_ge(slots_ready, k + 1)
                pool.sem_inc(passed_pool)
                for t in range(G):
                    for e in range(TOPK):
                        nc.gpsimd.indirect_dma_start(
                            out=sorted_rows,
                            out_offset=bass.IndirectOffsetOnAxis(ap=slot[:, r, e, t:t + 1], axis=0),
                            in_=pay[:, r, t, :], in_offset=None).then_inc(scattered[r], 16)

            turns(pool, turn)

            def add(j, s):
                pool.wait_ge(y_ready, j + 1 + Y_READY0)
                pool.wait_ge(y_added, 16 * j + Y_ADDED0)
                pool.sem_inc(passed_pool)
                nc.gpsimd.indirect_dma_start(
                    out=out, out_offset=bass.IndirectOffsetOnAxis(ap=xt[:, s, TOK:TOK + 1].bitcast(I32), axis=0),
                    in_=y[:, s % 2, :], in_offset=None, compute_op=ALU.add).then_inc(y_added, 16)

            with pool.Fori(0, TILES // XR) as i:
                for s in range(XR):
                    add(XR * i + s, s)
            last_tiles(pool, lambda j: add(j, j % XR))

        @block.scalar
        def _(act):
            act.sem_inc(y_ready, Y_READY0)
            def load(dst, src):
                act.dma_start(dst, src).then_inc(values_loaded, 16)

            load(wT_sb[:, :, 0:D], wT.rearrange("(c p) d -> p c d", p=P))
            load(ctxT_sb[:], ctxT.rearrange("(c p) k -> p c k", p=P))
            load(brow[0:1, 0:D], b_row)
            load(w_sb[:], w_rows.rearrange("(c p) d -> p c d", p=P))
            load(bcol[:], b_col)
            act.wait_ge(small_loaded, SMALL)
            nc.scalar.activation(gates[:], graw[:], ACT.Tanh).then_inc(gates_ready, 1)
            nc.scalar.preload_act_table_set("natural_log_exp_and_others")
            for b in range(BATCH):
                act.wait_ge(vw_ready, b + 1)
                nc.scalar.copy(vw[:, b, 0:D], O[0:CTX, b, 0:D]).then_inc(vw_copied, 1)
            for b, bank in enumerate((S[:, 0], S[:, 1], ET, R)):
                act.wait_ge(krT_ready, b + 1)
                nc.scalar.copy(krT[:, b], bank[:, 0:DC * KR].rearrange("p (c k) -> p c k", c=DC)).then_inc(krT_copied, 1)
            act.wait_ge(wr_ready, 1)
            nc.scalar.copy(brow[0:1, D:OW], R[0:1, 0:NE])
            nc.scalar.copy(wT_sb[:, :, D:OW], ET[:, 0:DC * NE].rearrange("p (c k) -> p c k", c=DC)).then_inc(wr_copied, 1)

            def inverse_sqrt(k, r):
                act.wait_ge(var_ready, k + 3)
                nc.scalar.activation(lnv[:], ve[:, r], ACT.Ln).then_inc(ln_ready, 1)
                act.wait_ge(ln_ready, k + 3)
                nc.scalar.activation(rt0[:], lnv[:], ACT.Exp, scale=-0.5).then_inc(rsqrt_ready, 1)

            def exponentials(g, r):
                act.wait_ge(negmax_ready, g + 1)
                for t in range(G):
                    last = nc.scalar.activation(ex[:, r, t], sm[:, r, t], ACT.Exp, bias=nb[:, r, t:t + 1],
                                                scale=rt[:, r, t:t + 1], accum_out=rs[:, r, t:t + 1])
                last.then_inc(exp_ready, 1)

            def copy_expT(g):
                act.wait_ge(expT_ready, g + 1)
                nc.scalar.copy(eT[:], ET[0:CTX, :]).then_inc(expT_copied, 1)

            for g in range(2):
                inverse_sqrt(g - 2, g)
                if g == 0:
                    act.wait_ge(vw_ready, BATCH + 1)
                    nc.scalar.copy(vw[:, :, D:OW], O[0:CTX, :, D:OW]).then_inc(vw_copied, 1)
                exponentials(g, g)
                copy_expT(g)

            def turn(k, r, i, behind):
                def norm(t):
                    rows = xg[:, bass.ds(slot_of(r, i) + t, 1), :].rearrange("p t d -> p (t d)")
                    return nc.scalar.activation(pay[:, r, t, 0:D], rows, ACT.Identity,
                                                bias=nmr2[:, r, t:t + 1], scale=rstd2[:, r, t:t + 1])

                inverse_sqrt(k, r)
                if behind > 1:
                    exponentials(k + 2, r)
                act.wait_ge(gap_ready, k + 1)
                nc.scalar.activation(ed[:], dl[:], ACT.Exp, scale=float(D) ** 0.5).then_inc(gap_exp_ready, 1)
                act.wait_ge(bias2_ready, k + 1)
                act.wait_ge(scattered[r], 16 * TOPK * G * i + SCATTERED0)
                norm(0)
                norm(1)
                if behind > 1:
                    copy_expT(k + 2)
                norm(2)
                norm(3)
                nc.scalar.copy(pay[:, r, :, TOK].bitcast(I32), tok[:, bass.ds(k * G, G)]).then_inc(rows_normed, 1)

            turns(act, turn)

            def cut_high(e, h, at, size):
                return nc.scalar.copy(w_high[h][:, bass.ds(e * HW + at, size)],
                                      raw[h][:, bass.ds(e, 1), at:at + size].rearrange("p e n -> p (e n)"))

            def cut_all_high(e):
                for h in range(HALVES):
                    last = cut_high(e, h, 0, HW)
                last.then_inc(weight_high, 1)

            act.wait_ge(raw_loaded, 16 * HALVES * EARLY)
            cut_all_high(0)

            def tile_highs(j, s):
                act.wait_ge(tileT_ready, j + 1)
                nc.scalar.copy(xtT[:, s % 2, 0], XT[:, s % 2, 0:D]).then_inc(tile_high, 1)

            def silu(j, s):
                act.wait_ge(gate_ready, j + 1)
                nc.scalar.activation(hid[:], GT[:], ACT.Silu).then_inc(silu_ready, 1)

            def hidden_highs(j):
                act.wait_ge(hiddenT_ready, j + 1)
                nc.scalar.copy(hT[:, 0], HT[:]).then_inc(hidden_high, 1)

            def weigh(j, s, e):
                act.wait_ge(down_ready, j + 1)
                act.wait_ge(y_added, 16 * (j - 1) + Y_ADDED0)
                nc.scalar.mul(y[:, s % 2], Y[:, s % 2, 0:D], xt[:, s, bass.ds(e + CW, 1)]).then_inc(y_ready, 1)

            act.wait_ge(tables_ready, 1)
            is_skewed = act.value_load(skewed[:], min_val=0, max_val=1)
            with act.If(is_skewed == 1):
                act.wait_ge(raw_late, 16 * HALVES * (NE - EARLY) + RAW_LATE0)
                for r in range(2):
                    act.wait_ge(scattered[r], SCATTERED0 + 16 * TOPK * G * HALF)
                    act.wait_ge(x2_stored[r], 16 * HALF + X2_STORED0)
                for e in range(1, NE):
                    cut_all_high(e)
            tile_highs(0, 0)
            tile_highs(1, 1)
            silu(0, 0)

            def turn(j, s, after=2, piece_of=None):
                hidden_highs(j)
                e = act.value_load(tile_expert[0:1, bass.ds(j, 1)], min_val=0, max_val=NE - 1)
                if after > 0:
                    silu(j + 1, s + 1)
                if after > 1:
                    tile_highs(j + 2, s + 2)
                if piece_of is not None:
                    with act.If(is_skewed == 0):
                        at = s % CUTS * PIECE
                        cut_high(piece_of, at // HW, at % HW, PIECE).then_inc(weight_high, 1)
                weigh(j, s, e)

            with act.Fori(0, NE // 2 - 1) as i:
                act.wait_ge(raw_late, 16 * HALVES * 2 * i + RAW_LATE0)
                act.sem_inc(passed_act)
                for s in range(XR):
                    turn(XR * i + s, s, piece_of=2 * i + 1 + s // CUTS)
            act.wait_ge(raw_late, 16 * HALVES * (NE - EARLY) + RAW_LATE0)
            for s in range(XR):
                turn(XR * (NE // 2 - 1) + s, s, piece_of=NE - 1 if s < CUTS else None)
            with act.Fori(NE // 2, TURNS) as i:
                for s in range(XR):
                    turn(XR * i + s, s)
            last_tiles(act, lambda j: turn(j, j % XR, TILES - 1 - j))

        @block.vector
        def _(dve):
            tt, ts, stt = nc.vector.tensor_tensor, nc.vector.tensor_scalar, nc.vector.scalar_tensor_tensor

            def per_expert(v):
                return v.unsqueeze(2).to_broadcast([P, G, NE])

            def per_tile(v):
                return v.unsqueeze(1).to_broadcast([P, G, NE])

            nc.vector.memset(kr[:], 0.0).then_inc(kr_zeroed, 1)
            nc.vector.memset(carry[:], 0.0)
            nc.vector.memset(ve[:], 1.0)
            nc.vector.memset(ones_row[:], 1.0).then_inc(setup_steps, 1)
            dve.wait_ge(setup_steps, 1)
            dve.wait_ge(keys_loaded, KEYS)
            for b in range(BATCH):
                last = nc.vector.bn_stats(kst[:, b], kr[:, b])
            last.then_inc(setup_steps, 1)
            dve.wait_ge(setup_steps, 2)
            for b in range(BATCH):
                last = nc.vector.bn_aggr(kmv[:, b], kst[:, b])
            last.then_inc(setup_steps, 1)
            dve.wait_ge(setup_steps, 3)
            for b in range(BATCH):
                ts(kr[:, b], kr[:, b], kmv[:, b, 0:1], None, ALU.subtract).then_inc(keys_centred, 1)
            dve.wait_ge(small_loaded, SMALL)
            nc.vector.tensor_copy(lens_f[:], lens_i[:]).then_inc(setup_steps, 1)
            dve.wait_ge(setup_steps, 4)
            dve.wait_ge(pool_consts, 8)
            for b in range(BATCH):
                ts(kmask[:, b * CTX:(b + 1) * CTX], kpos[:], lens_f[:, b:b + 1], MASKED, ALU.is_ge, ALU.mult)
                last = ts(qmask[:, b * QT:(b + 1) * QT], qpos[:], lens_f[:, b:b + 1], None, ALU.is_ge)
            last.then_inc(setup_steps, 1)
            dve.wait_ge(setup_steps, 5)
            dve.wait_ge(gates_ready, 1)

            base = [0, 0]

            def mark(ins):
                base[1] += 1
                ins.then_inc(dve_steps, 1)
                return base[1]

            def after(step):
                dve.wait_ge(dve_steps, base[0] + step)

            def rows(r, i, t):
                return xg[:, bass.ds(slot_of(r, i) + t, 1), :].rearrange("p t d -> p (t d)")

            def statistics(st, r, i, tiles=range(G)):
                for t in tiles:
                    last = nc.vector.bn_stats(st[:, t], rows(r, i, t))
                return last

            def aggregates(which, st):
                dve.sem_inc(passed_dve)
                for t in range(G):
                    last = nc.vector.bn_aggr(mv[:, which, t], st[:, t])
                return last

            def variances(r, norms):
                return ts(ve[:, r, 0:norms * G].rearrange("p (w t) -> p w t", w=norms), mv[:, 0:norms, :, 1],
                          EPS, float(D), ALU.add, ALU.mult).then_inc(var_ready, 1)

            def masked_scores(g, q, b):
                dve.wait_ge(scores_ready, g + 1)
                for t in range(G):
                    last = stt(out=sm[:, q, t], in0=kmask[:, bass.ds(b * CTX, CTX)],
                               scalar=qmask[:, bass.ds(g * G + t, 1)],
                               in1=S[:, q, t * KR:t * KR + CTX], op0=ALU.mult, op1=ALU.add)
                return last

            def router_part(q):
                nc.vector.tensor_copy(
                    sr[:, q], S[:, q, 0:G * KR].rearrange("p (t k) -> p t k", t=G)[:, :, CTX:CTX + NE]
                ).then_inc(scores_free, 1)

            def refine(k, r, meanwhile=None):
                dve.wait_ge(rsqrt_ready, k + 3)
                half = mark(stt(out=rt0v[:], in0=rt0[:], scalar=-0.5, in1=ve[:, r], op0=ALU.mult, op1=ALU.mult))
                if meanwhile is not None:
                    meanwhile()
                after(half)
                after(mark(tt(out=rt0c[:], in0=rt0v[:], in1=rt0[:], op=ALU.mult)))
                return mark(stt(out=rt[:, r], in0=rt0c[:], scalar=1.5, in1=rt0[:], op0=ALU.add, op1=ALU.mult))

            def maxima(q):
                nc.vector.tensor_reduce(mx[:], sm[:, q], axis=AX.X, op=ALU.max)

            def negated_maxima(q):
                stt(out=nb[:, q], in0=mx[:], scalar=-1.0, in1=rt[:, q, 0:G],
                    op0=ALU.mult, op1=ALU.mult).then_inc(negmax_ready, 1)

            for g in range(2):
                dve.wait_ge(x_loaded[g], 16)
                after(mark(statistics(st1, g, 0)))
                after(mark(aggregates(0, st1)))
                variances(g, 1)
                scores0 = mark(masked_scores(g, g, 0))
                router_part(g)
                after(scores0)
                maxima(g)
                after(refine(g - 2, g))
                negated_maxima(g)
            first = base[1]

            def turn(k, r, i, behind):
                base[0] = base[0] + base[1] if behind == 0 else k * STEPS + first
                base[1] = 0
                dve.wait_ge(exp_ready, k + 1)
                inv = mark(nc.vector.reciprocal(rg[:], rs[:, r]))
                if behind > 1:
                    dve.wait_ge(x_loaded[r], 16 * (i + 1) + 16)
                    dve.sem_inc(passed_dve)
                    stats1 = mark(statistics(st1, r, i + 1))
                after(inv)
                factor = mark(ts(rgt[:], rg[:], gates[:, 0:1], None, ALU.mult))
                if behind > 1:
                    after(stats1)
                    mark(aggregates(0, st1))
                after(factor)
                dve.wait_ge(attn_ready, k + 1)
                tt(out=lg0[:], in0=O[:, :, D:OW], in1=per_expert(rgt[:]), op=ALU.mult)
                added = [stt(out=rows(r, i, t), in0=O[:, t, 0:D], scalar=rgt[:, t:t + 1], in1=rows(r, i, t),
                             op0=ALU.mult, op1=ALU.add) for t in range(G)]
                half = mark(added[G // 2 - 1])
                added[-1].then_inc(attn_used, 1)
                after(half)
                dve.sem_inc(passed_dve)
                statistics(st2, r, i, range(G // 2))
                dve.wait_ge(attn_used, k + 1)
                dve.sem_inc(passed_dve)
                stats2 = mark(statistics(st2, r, i, range(G // 2, G)))
                tt(out=lg1[:], in0=lg0[:], in1=sr[:, r], op=ALU.add)
                after(stats2)
                after(mark(aggregates(1, st2)))
                variances(r, 2)
                if behind > 1:
                    scores = mark(masked_scores(k + 2, r, i + 1))
                    router_part(r)

                    def reduced():
                        after(scores)
                        maxima(r)

                    refined = refine(k, r, reduced)
                else:
                    refined = refine(k, r)
                after(refined)
                if behind > 1:
                    negated_maxima(r)
                logits = mark(tt(out=lg[:], in0=lg1[:], in1=per_expert(rt[:, r, G:2 * G]), op=ALU.mult))
                root = mark(ts(rstd2[:, r], rt[:, r, G:2 * G], float(D) ** 0.5, None, ALU.mult))
                after(logits)
                dve.sem_inc(passed_dve)
                for t in range(G):
                    last = nc.vector.max(m8[:, t], lg[:, t])
                largest = mark(last)
                after(root)
                stt(out=nmr2[:, r], in0=mv[:, 1, :, 0], scalar=-1.0, in1=rstd2[:, r],
                    op0=ALU.mult, op1=ALU.mult).then_inc(bias2_ready, 1)
                after(largest)
                tt(out=dl[:], in0=m8[:, :, 1], in1=m8[:, :, 0], op=ALU.subtract).then_inc(gap_ready, 1)
                for t in range(G):
                    last = nc.vector.max_index(mi[:, t], m8[:, t], lg[:, t])
                after(mark(last))
                both = [P, TOPK, G, NE]
                after(mark(tt(out=oh[:], in0=iota_e[:].unsqueeze(1).unsqueeze(1).to_broadcast(both),
                              in1=mi[:, :, 0:TOPK].rearrange("p t e -> p e t").unsqueeze(3).to_broadcast(both),
                              op=ALU.is_equal)))
                tt(out=picks[:], in0=oh[:, 0], in1=oh[:, 1], op=ALU.add).then_inc(picks_ready, 1)
                dve.wait_ge(gap_exp_ready, k + 1)
                above = mark(ts(ed1[:], ed[:], 1.0, None, ALU.add))
                dve.wait_ge(ranks_ready, k + 1)
                places = mark(tt(out=place[:], in0=R[:, 0:G * NE].rearrange("p (t e) -> p t e", t=G),
                                 in1=per_tile(region[:]), op=ALU.add))
                after(above)
                share = mark(nc.vector.reciprocal(rw[:], ed1[:]))
                after(places)
                own = mark(tt(out=po[:], in0=oh[:], in1=place[:].unsqueeze(1).to_broadcast(both), op=ALU.mult))
                after(share)
                first_w = mark(ts(wk[:, 0], rw[:], gates[:, 1:2], None, ALU.mult))
                after(own)
                dve.wait_ge(scattered[r], 16 * TOPK * G * i + SCATTERED0)
                with nc.allow_low_precision(reason="whole numbers below 2**24, summed in float32"):
                    nc.vector.tensor_reduce(slot[:, r], po[:], axis=AX.X, op=ALU.add)
                after(first_w)
                second_w = mark(tt(out=wk[:, 1], in0=wk[:, 0], in1=ed[:], op=ALU.mult))
                dve.wait_ge(picks_ready, k + 1)
                counted = mark(nc.vector.tensor_reduce(npicks[:], picks[:].rearrange("p t e -> p e t"),
                                                       axis=AX.X, op=ALU.add))
                after(second_w)
                weighed = mark(tt(out=cw[:], in0=oh[:], in1=wk[:].unsqueeze(3).to_broadcast(both), op=ALU.mult))
                after(counted)
                carried = mark(tt(out=carry[:], in0=carry[:], in1=npicks[:], op=ALU.add))
                after(weighed)
                tt(out=pay[:, r, :, CW:ROW], in0=cw[:, 0], in1=cw[:, 1], op=ALU.add).then_inc(slots_ready, 1)
                assert behind < 2 or base[1] == STEPS, base[1]

            turns(dve, turn)

            done = [0]

            def step(ins):
                done[0] += 1
                ins.then_inc(table_steps, 1)
                dve.wait_ge(table_steps, done[0])

            dve.wait_ge(counts_ready, 1)
            nc.vector.tensor_copy(cnt[:], R[0:1, 0:NE])
            step(ts(nti[:], R[0:1, 0:NE], float(P - 1), None, ALU.add))
            tt(out=pad_row[:], in0=region[0:1, :], in1=cnt[:], op=ALU.add).then_inc(pad_rows_ready, 1)
            step(nc.vector.tensor_single_scalar(nts[:], nti[:], P.bit_length() - 1, ALU.logical_shift_right))
            step(nc.vector.tensor_copy(ntf[:], nts[:]))
            step(nc.vector.tensor_tensor_scan(cum[:], one8[:], ntf[:], 0.0, ALU.mult, ALU.add))
            tt(out=start[:], in0=cum[:], in1=ntf[:], op=ALU.subtract)
            step(tt(out=past[:], in0=J[:].unsqueeze(2).to_broadcast([1, TILES, NE]),
                    in1=cum[:].unsqueeze(1).to_broadcast([1, TILES, NE]), op=ALU.is_ge))
            tt(out=soon[:], in0=start[:], in1=need[:], op=ALU.is_lt)
            nc.vector.tensor_reduce(tex[:], past[:], axis=AX.X, op=ALU.add)
            step(tt(out=pastn[:], in0=past[:], in1=ntf[:].unsqueeze(1).to_broadcast([1, TILES, NE]), op=ALU.mult))
            nc.vector.tensor_reduce(skew_f[:], soon[0:1, 1:NE], axis=AX.X, op=ALU.max)
            step(nc.vector.tensor_reduce(before[:], pastn[:], axis=AX.X, op=ALU.add))
            nc.vector.tensor_copy(skewed[:], skew_f[:])
            step(tt(out=rel[:], in0=J[:], in1=before[:], op=ALU.subtract))
            step(ts(rel128[:], rel[:], float(P), None, ALU.mult))
            ts(tile_expert[:], tex[:], float(NE - 1), None, ALU.min)
            nc.vector.tensor_copy(tiles_used[:], cum[0:1, NE - 1:NE])
            stt(out=tile_row[:], in0=tex[:], scalar=float(REGION), in1=rel128[:],
                op0=ALU.mult, op1=ALU.add).then_inc(tables_ready, 1)

            def cut_low(e, h, at, size):
                return tt(out=w_low[h][:, bass.ds(e * HW + at, size)],
                          in0=raw[h][:, bass.ds(e, 1), at:at + size].rearrange("p e n -> p (e n)"),
                          in1=w_high[h][:, bass.ds(e * HW + at, size)].bitcast(F32), op=ALU.subtract)

            def cut_all_low(e):
                dve.wait_ge(weight_high, e + 1)
                for h in range(HALVES):
                    last = cut_low(e, h, 0, HW)
                last.then_inc(weight_low, 1)

            cut_all_low(0)

            def tile_lows(j, s):
                dve.wait_ge(tile_high, j + 1)
                tt(out=xtT[:, s % 2, 1], in0=XT[:, s % 2, 0:D], in1=xtT[:, s % 2, 0].bitcast(F32),
                   op=ALU.subtract).then_inc(tile_low, 1)

            def gate_up(j, s):
                dve.wait_ge(up_ready, j + 1)
                tt(out=hid[:], in0=hid[:], in1=UP[:], op=ALU.mult).then_inc(hidden_ready, 1)

            def hidden_lows(j):
                dve.wait_ge(hidden_high, j + 1)
                tt(out=hT[:, 1], in0=HT[:], in1=hT[:, 0].bitcast(F32), op=ALU.subtract).then_inc(hidden_low, 1)

            is_skewed = dve.value_load(skewed[:], min_val=0, max_val=1)
            with dve.If(is_skewed == 1):
                for e in range(1, NE):
                    cut_all_low(e)
            tile_lows(0, 0)
            tile_lows(1, 1)
            dve.wait_ge(silu_ready, 1)
            gate_up(0, 0)

            def turn(j, s, after=2, piece_of=None):
                hidden_lows(j)
                if after > 1:
                    tile_lows(j + 2, s + 2)
                if after == 1:
                    dve.wait_ge(silu_ready, j + 2)
                if after > 0:
                    gate_up(j + 1, s + 1)
                if piece_of is not None:
                    with dve.If(is_skewed == 0):
                        dve.wait_ge(weight_high, j + 2)
                        at = s % CUTS * PIECE
                        last = cut_low(piece_of, at // HW, at % HW, PIECE)
                        if s % CUTS == CUTS - 1:
                            last.then_inc(weight_low, 1)

            with dve.Fori(0, NE // 2 - 1) as i:
                for s in range(XR):
                    turn(XR * i + s, s, piece_of=2 * i + 1 + s // CUTS)
            for s in range(XR):
                turn(XR * (NE // 2 - 1) + s, s, piece_of=NE - 1 if s < CUTS else None)
            with dve.Fori(NE // 2, TURNS) as i:
                for s in range(XR):
                    turn(XR * i + s, s)
            last_tiles(dve, lambda j: turn(j, j % XR, TILES - 1 - j))

        @block.tensor
        def _(pe):
            mm = nc.tensor.matmul
            pe.wait_ge(values_loaded, VALUES)
            pe.wait_ge(setup_steps, 1)

            def carried(b, columns):
                for c in range(DC):
                    mm(O[0:CTX, b, columns], ctxT_sb[:, c, b * CTX:(b + 1) * CTX], wT_sb[:, c, columns],
                       start=(c == 0), stop=False)
                return mm(O[0:CTX, b, columns], ones_row[:], brow[:, columns], start=False, stop=True)

            for b in range(BATCH):
                carried(b, slice(0, D)).then_inc(vw_ready, 1)
            pe.wait_ge(pool_consts, 2)
            for b, bank in enumerate((S[:, 0], S[:, 1], ET, R)):
                pe.wait_ge(keys_centred, b + 1)
                for c in range(DC):
                    last = nc.tensor.transpose(bank[:, c * KR:(c + 1) * KR], kr[:, b, c * P:(c + 1) * P],
                                               ident[0:KR, 0:KR])
                last.then_inc(krT_ready, 1)
            pe.wait_ge(krT_copied, BATCH)

            def scores(g, r, b):
                for t in range(G):
                    for c in range(DC):
                        last = mm(S[:, r, t * KR:(t + 1) * KR], xTg[:, r, c, t * P:(t + 1) * P],
                                  krT[:, bass.ds(b, 1), c, :].rearrange("p b k -> p (b k)"),
                                  start=(c == 0), stop=(c == DC - 1))
                last.then_inc(scores_ready, 1)

            routerT = krT[:, 0, :, CTX:CTX + NE]
            for dc in range(DC):
                for c in range(DC):
                    mm(ET[:, dc * NE:(dc + 1) * NE], w_sb[:, c, dc * P:(dc + 1) * P], routerT[:, c],
                       start=(c == 0), stop=(c == DC - 1))
            for c in range(DC):
                last = mm(R[0:1, 0:NE], bcol[:, c:c + 1], routerT[:, c], start=(c == 0), stop=(c == DC - 1))
            last.then_inc(wr_ready, 1)
            pe.wait_ge(xT_loaded[0], 16)
            scores(0, 0, 0)
            pe.wait_ge(wr_copied, 1)
            pe.wait_ge(vw_copied, BATCH)
            for b in range(BATCH):
                last = carried(b, slice(D, OW))
            last.then_inc(vw_ready, 1)
            pe.wait_ge(xT_loaded[1], 16)
            scores(1, 1, 0)
            pe.wait_ge(vw_copied, BATCH + 1)

            def transpose_exp(g, r):
                pe.wait_ge(exp_ready, g + 1)
                for t in range(G):
                    last = nc.tensor.transpose(ET[0:CTX, t * P:(t + 1) * P], ex[:, r, t], ident[:])
                last.then_inc(expT_ready, 1)

            def attention(g, b):
                pe.wait_ge(expT_copied, g + 1)
                for t in range(G):
                    last = mm(O[:, t, 0:OW], eT[:, t * P:(t + 1) * P],
                              vw[:, bass.ds(b, 1), :].rearrange("p b k -> p (b k)"), start=True, stop=True)
                last.then_inc(attn_ready, 1)

            transpose_exp(0, 0)
            attention(0, 0)
            transpose_exp(1, 1)

            def turn(k, r, i, behind):
                if behind > 1:
                    pe.wait_ge(xT_loaded[r], 16 * i + 32)
                    pe.wait_ge(scores_free, k + 1)
                    scores(k + 2, r, i + 1)
                if behind > 0:
                    pe.wait_ge(attn_used, k + 1)
                    attention(k + 1, i + r)
                pe.wait_ge(picks_ready, k + 1)
                ranks = R[:, 0:G * NE].rearrange("p (t e) -> p t e", t=G)
                mm(ranks, ones[:], carry[:].unsqueeze(1).to_broadcast([P, G, NE]), start=True, stop=False)
                for t in range(G - 1):
                    mm(ranks[:, t + 1:G], ones[:], picks[:, t:t + 1].to_broadcast([P, G - 1 - t, NE]),
                       start=False, stop=False, skip_group_check=True)
                mm(ranks, tri[:], picks[:], start=False, stop=True).then_inc(ranks_ready, 1)
                if behind > 1:
                    transpose_exp(k + 2, r)

            turns(pe, turn)

            pe.wait_ge(slots_ready, GROUPS)
            mm(R[:, 0:NE], ones[:], carry[:], start=True, stop=True).then_inc(counts_ready, 1)

            def expert(j):
                return pe.value_load(tile_expert[0:1, bass.ds(j, 1)], min_val=0, max_val=NE - 1)

            def transpose_tile(s):
                for c in range(DC):
                    last = nc.tensor.transpose(XT[:, s % 2, c * P:(c + 1) * P], xt[:, s % XR, c * P:(c + 1) * P], ident[:])
                last.then_inc(tileT_ready, 1)

            parts = (w_high, w_low)
            HI_LO = ((0, 0), (0, 1), (1, 0))

            def first_layer(bank, s, e, k):
                for c in range(DC):
                    for n, (px, pw) in enumerate(HI_LO):
                        last = mm(bank[:], xtT[:, s % 2, px, c * P:(c + 1) * P],
                                  parts[pw][c][:, bass.ds(e * HW + k * HID, HID)],
                                  start=(c == 0 and n == 0), stop=(c == DC - 1 and n == 2))
                return last

            def gate(j, s, e):
                pe.wait_ge(tile_low, j + 1)
                first_layer(GT, s, e, 0).then_inc(gate_ready, 1)

            def up(j, s, e):
                first_layer(UP, s, e, 1).then_inc(up_ready, 1)

            def transpose_hidden(j, s):
                pe.wait_ge(hidden_ready, j + 1)
                for c in range(HC):
                    last = nc.tensor.transpose(HT[:, c * P:(c + 1) * P], hid[:, c * P:(c + 1) * P], ident[:])
                last.then_inc(hiddenT_ready, 1)

            def down(j, s, e):
                pe.wait_ge(hidden_low, j + 1)
                for px in range(2):
                    for c in range(HC):
                        for pw in range(2 - px):
                            last = mm(Y[:, s % 2, 0:D], hT[:, px, c * P:(c + 1) * P],
                                      parts[pw][c // (HC // DC)][:, bass.ds(e * HW + DOWN + c % (HC // DC) * D, D)],
                                      start=(px == 0 and c == 0 and pw == 0), stop=(px == 1 and c == HC - 1))
                last.then_inc(down_ready, 1)

            def turn(j, s, turns, e=None, e1=None, after=2):
                e2 = None
                transpose_hidden(j, s)
                if after > 0:
                    if e1 is None:
                        e1 = expert(j + 1)
                    gate(j + 1, s + 1, e1)
                if after > 1:
                    pe.wait_ge(tile_loaded[(s + 2) % XR], 16 * (turns + 1 + (s + 2) // XR))
                    transpose_tile(s + 2)
                if after > 0:
                    up(j + 1, s + 1, e1)
                if after > 1:
                    e2 = expert(j + 2)
                if e is None:
                    e = expert(j)
                down(j, s, e)
                return e1, e2

            pe.wait_ge(tables_ready, 1)
            e = expert(0)
            for j in range(2):
                pe.wait_ge(tile_loaded[j], 16)
                transpose_tile(j)
            gate(0, 0, e)
            up(0, 0, e)
            with pe.Fori(0, TURNS) as i:
                e, e1 = None, None
                for s in range(XR):
                    e, e1 = turn(XR * i + s, s, i, e, e1)
            known = [None, None]

            def tile(j):
                known[:] = turn(j, j % XR, TURNS, *known, TILES - 1 - j)

            last_tiles(pe, tile)


def kernel(x, ctx_1024, _lenS2, g_xattn, g_ffn, L0_xattn_W, L0_xattn_b, L0_ffn_router_w, L0_ffn_w_gate,
           L0_ffn_w_up, L0_ffn_w_down):
    import numpy as np
    import concourse.bacc as bacc
    from concourse.bass_utils import run_bass_kernel_spmd

    rows = np.asarray(x).reshape(N, D)
    ctx = np.asarray(ctx_1024)
    W = np.asarray(L0_xattn_W)
    b = np.asarray(L0_xattn_b)

    def by_chunk(w):
        e, rows_, cols = w.shape
        return w.reshape(e, rows_ // P, P, cols).transpose(0, 2, 1, 3)

    gate, up, down = (by_chunk(np.asarray(w).transpose(0, 2, 1)) for w in (L0_ffn_w_gate, L0_ffn_w_up, L0_ffn_w_down))
    weights = np.concatenate([np.stack([gate, up], axis=3).reshape(NE, P, HALVES, DOWN),
                              down.reshape(NE, P, HALVES, HW - DOWN)], axis=3)
    laid_out = {
        "x": rows, "xT": rows.T,
        "ctx_rows": ctx, "ctxT": ctx.reshape(BATCH * CTX, D).T,
        "lens": np.asarray(_lenS2).reshape(1, BATCH),
        "g_x": np.asarray(g_xattn).reshape(1, 1), "g_f": np.asarray(g_ffn).reshape(1, 1),
        "w_rows": W, "wT": W.T, "b_row": b.reshape(1, D), "b_col": b.reshape(DC, P).T,
        "router": np.asarray(L0_ffn_router_w), "weights": weights,
    }
    nc = bacc.Bacc("TRN2", target_bir_lowering=False, num_devices=1, dynamic_dma_scratch_size=4096)
    arrays, args = {}, []
    for name, a in laid_out.items():
        a = np.ascontiguousarray(a)
        arrays[f"in_{name}"] = a
        args.append(nc.dram_tensor(f"in_{name}", a.shape, mybir.dt.from_np(a.dtype), kind="ExternalInput").ap())
    args.append(nc.dram_tensor("out_rows", (N + P, D), F32, kind="ExternalOutput").ap())
    moe_flamingo(nc, *args)
    r = run_bass_kernel_spmd(nc, [arrays], core_ids=[0])
    return r.results[0]["out_rows"][:N].reshape(BATCH, SEQ, D)
```
